# Optimizing a Trainium2 kernel written in Bass

```python
import numpy as np
import jax
import jax.numpy as jnp

def _softmax(x, axis=-1):
    return jax.nn.softmax(x, axis=axis)

def _gelu(x):
    return jax.nn.gelu(x, approximate=True)

def _silu(x):
    return jax.nn.silu(x)

def _sigmoid(x):
    return jax.nn.sigmoid(x)

def _layernorm(x, axis=-1, eps=1e-05):
    m = jnp.mean(x, axis=axis, keepdims=True)
    v = jnp.var(x, axis=axis, keepdims=True)
    return (x - m) / jnp.sqrt(v + eps)

def _scatter_add(tgt, idx, src, axis=0):
    return tgt.at[idx].add(src)

def _segment_sum(src, seg, n):
    return jax.ops.segment_sum(src, seg, n)
kernel_name = 'mk_gnn_resnorm_d2_gnn_r64_2a4d6d'

def setup_inputs(seed: int=0):
    np.random.seed(seed)
    _w = jnp.asarray

    def _rec_inputs():
        import jax
        import jax.numpy as jnp
        _gk = jax.random.key(seed)
        x = -0.0003929 + 0.9999 * jax.random.normal(jax.random.fold_in(_gk, 1), (512, 512), jnp.float32)
        src = jax.random.randint(jax.random.fold_in(_gk, 2), (16384,), 0, 512, jnp.int32)
        dst = jnp.minimum((512 * jax.random.uniform(jax.random.fold_in(_gk, 3), (16384,)) ** 2.0).astype(jnp.int32), 32767)
        _o = jnp.argsort(dst, stable=True)
        src = src[_o]
        dst = dst[_o]
        edge_attr_8 = -4.48278e-06 + 1.00019 * jax.random.normal(jax.random.fold_in(_gk, 12), (16384, 8), jnp.float32)
        edge_type_2 = jax.random.randint(jax.random.fold_in(_gk, 14), (16384,), 0, 2, jnp.int32)
        return (x, src, dst, edge_attr_8, edge_type_2)
    x, src, dst, edge_attr_8, edge_type_2 = _rec_inputs()

    def _L0_gnn_setup():
        import jax, jax.numpy as jnp
        import numpy as np
        L, C, H, E = (512, 512, 8, 16384)
        D = C // H
        HID = 1024
        EPS = 1e-05

        def _ln(x, g, b):
            mu = jnp.mean(x, axis=-1, keepdims=True)
            var = jnp.var(x, axis=-1, keepdims=True)
            return (x - mu) * jax.lax.rsqrt(var + EPS) * g + b

        def _sparse_attention(z, row, col, bias, Wq, bq, Wk, bk, Wv, bv, Wo, bo):
            q = (z @ Wq + bq).reshape(L, H, D)
            k = (z @ Wk + bk).reshape(L, H, D)
            v = (z @ Wv + bv).reshape(L, H, D)
            scale = 1.0 / jnp.sqrt(jnp.asarray(D, z.dtype))
            scores = jnp.einsum('ehd,ehd->eh', q[row], k[col]) * scale + bias
            m = jax.ops.segment_max(scores, row, num_segments=L)
            p = jnp.exp(scores - m[row])
            ssum = jax.ops.segment_sum(p, row, num_segments=L)
            alpha = p / ssum[row]
            out = jax.ops.segment_sum(alpha[:, :, None] * v[col], row, num_segments=L)
            return out.reshape(L, C) @ Wo + bo
        key = jax.random.key(seed)
        ks = jax.random.split(key, 12)
        s = 0.02
        inp = {'x': jax.random.normal(ks[0], (L, C), jnp.float32), 'row_index': jnp.sort(jax.random.randint(ks[1], (E,), 0, L)), 'col_index': jax.random.randint(ks[2], (E,), 0, L), 'att_bias': jax.random.normal(ks[3], (E, H), jnp.float32), 'Wq': jax.random.normal(ks[4], (C, C), jnp.float32) * s, 'bq': jnp.zeros((C,), jnp.float32), 'Wk': jax.random.normal(ks[5], (C, C), jnp.float32) * s, 'bk': jnp.zeros((C,), jnp.float32), 'Wv': jax.random.normal(ks[6], (C, C), jnp.float32) * s, 'bv': jnp.zeros((C,), jnp.float32), 'Wo': jax.random.normal(ks[7], (C, C), jnp.float32) * s, 'bo': jnp.zeros((C,), jnp.float32), 'ln1_g': jnp.ones((C,), jnp.float32), 'ln1_b': jnp.zeros((C,), jnp.float32), 'ln2_g': jnp.ones((C,), jnp.float32), 'ln2_b': jnp.zeros((C,), jnp.float32), 'W1': jax.random.normal(ks[8], (C, HID), jnp.float32) * s, 'b1': jnp.zeros((HID,), jnp.float32), 'W2': jax.random.normal(ks[9], (HID, C), jnp.float32) * s, 'b2': jnp.zeros((C,), jnp.float32)}
        return inp
    _L0_gnn_all = _L0_gnn_setup()
    _L0_gnn_in = {k: v for k, v in _L0_gnn_all.items() if k in ('Wq', 'bq', 'Wk', 'bk', 'Wv', 'bv', 'Wo', 'bo', 'ln1_g', 'ln1_b', 'ln2_g', 'ln2_b', 'W1', 'b1', 'W2', 'b2')}
    del _L0_gnn_all

    def _L1_gnn_setup():
        import jax, jax.numpy as jnp
        import numpy as np
        NUM_RELATIONS = 2
        NUM_BASES = 30
        HIDDEN = 512
        N_NODES = 10000
        N_EDGES = 2500

        def rgcn_gate_layer(x, row, col, edge_type, basis, att, gate_w, root, bias):
            H = x.shape[1]
            w = jnp.einsum('rb,bio->rio', att, basis)
            x_j = x[col]
            msgs = []
            for r in range(NUM_RELATIONS):
                gate = jax.nn.sigmoid(x_j @ gate_w[r, :, 0])
                msgs.append(gate[:, None] * x_j @ w[r])
            msg = jnp.where((edge_type == 0)[:, None], msgs[0], msgs[1])
            agg = jax.ops.segment_sum(msg, row, num_segments=x.shape[0])
            return agg + x @ root + bias
        key = jax.random.key(seed)
        ks = jax.random.split(key, 16)
        H, R, B = (HIDDEN, NUM_RELATIONS, NUM_BASES)
        bound = 1.0 / np.sqrt(B * H)
        u = lambda k, shape: jax.random.uniform(k, shape, jnp.float32, -bound, bound)
        inp = {'x': jax.random.normal(ks[0], (N_NODES, H), jnp.float32), 'edge_index': jax.random.randint(ks[1], (2, N_EDGES), 0, N_NODES, jnp.int32), 'edge_type': jax.random.randint(ks[2], (N_EDGES,), 0, R, jnp.int32), 'basis1': u(ks[3], (B, H, H)), 'att1': u(ks[4], (R, B)), 'gate_w1': u(ks[5], (R, H, 1)), 'root1': u(ks[6], (H, H)), 'bias1': u(ks[7], (H,)), 'basis2': u(ks[8], (B, H, H)), 'att2': u(ks[9], (R, B)), 'gate_w2': u(ks[10], (R, H, 1)), 'root2': u(ks[11], (H, H)), 'bias2': u(ks[12], (H,))}
        return inp
    _L1_gnn_all = _L1_gnn_setup()
    _L1_gnn_in = {k: v for k, v in _L1_gnn_all.items() if k in ('basis1', 'att1', 'gate_w1', 'root1', 'bias1', 'basis2', 'att2', 'gate_w2', 'root2', 'bias2')}
    del _L1_gnn_all
    return {'x': x, 'src': src, 'dst': dst, 'edge_attr_8': edge_attr_8, 'edge_type_2': edge_type_2, 'L0_gnn_Wq': _L0_gnn_in['Wq'], 'L0_gnn_bq': _L0_gnn_in['bq'], 'L0_gnn_Wk': _L0_gnn_in['Wk'], 'L0_gnn_bk': _L0_gnn_in['bk'], 'L0_gnn_Wv': _L0_gnn_in['Wv'], 'L0_gnn_bv': _L0_gnn_in['bv'], 'L0_gnn_Wo': _L0_gnn_in['Wo'], 'L0_gnn_bo': _L0_gnn_in['bo'], 'L0_gnn_ln1_g': _L0_gnn_in['ln1_g'], 'L0_gnn_ln1_b': _L0_gnn_in['ln1_b'], 'L0_gnn_ln2_g': _L0_gnn_in['ln2_g'], 'L0_gnn_ln2_b': _L0_gnn_in['ln2_b'], 'L0_gnn_W1': _L0_gnn_in['W1'], 'L0_gnn_b1': _L0_gnn_in['b1'], 'L0_gnn_W2': _L0_gnn_in['W2'], 'L0_gnn_b2': _L0_gnn_in['b2'], 'L1_gnn_basis1': _L1_gnn_in['basis1'], 'L1_gnn_att1': _L1_gnn_in['att1'], 'L1_gnn_gate_w1': _L1_gnn_in['gate_w1'], 'L1_gnn_root1': _L1_gnn_in['root1'], 'L1_gnn_bias1': _L1_gnn_in['bias1'], 'L1_gnn_basis2': _L1_gnn_in['basis2'], 'L1_gnn_att2': _L1_gnn_in['att2'], 'L1_gnn_gate_w2': _L1_gnn_in['gate_w2'], 'L1_gnn_root2': _L1_gnn_in['root2'], 'L1_gnn_bias2': _L1_gnn_in['bias2']}

def reference(x, src, dst, edge_attr_8, edge_type_2, L0_gnn_Wq, L0_gnn_bq, L0_gnn_Wk, L0_gnn_bk, L0_gnn_Wv, L0_gnn_bv, L0_gnn_Wo, L0_gnn_bo, L0_gnn_ln1_g, L0_gnn_ln1_b, L0_gnn_ln2_g, L0_gnn_ln2_b, L0_gnn_W1, L0_gnn_b1, L0_gnn_W2, L0_gnn_b2, L1_gnn_basis1, L1_gnn_att1, L1_gnn_gate_w1, L1_gnn_root1, L1_gnn_bias1, L1_gnn_basis2, L1_gnn_att2, L1_gnn_gate_w2, L1_gnn_root2, L1_gnn_bias2):
    import jax
    import jax.numpy as jnp

    def _L0_gnn_ref(x, att_bias, Wq, bq, Wk, bk, Wv, bv, Wo, bo, ln1_g, ln1_b, ln2_g, ln2_b, W1, b1, W2, b2, row_index, col_index):
        import jax, jax.numpy as jnp
        import numpy as np
        L, C, H, E = (512, 512, 8, 16384)
        D = C // H
        HID = 1024
        EPS = 1e-05

        def _ln(x, g, b):
            mu = jnp.mean(x, axis=-1, keepdims=True)
            var = jnp.var(x, axis=-1, keepdims=True)
            return (x - mu) * jax.lax.rsqrt(var + EPS) * g + b

        def _sparse_attention(z, row, col, bias, Wq, bq, Wk, bk, Wv, bv, Wo, bo):
            q = (z @ Wq + bq).reshape(L, H, D)
            k = (z @ Wk + bk).reshape(L, H, D)
            v = (z @ Wv + bv).reshape(L, H, D)
            scale = 1.0 / jnp.sqrt(jnp.asarray(D, z.dtype))
            scores = jnp.einsum('ehd,ehd->eh', q[row], k[col]) * scale + bias
            m = jax.ops.segment_max(scores, row, num_segments=L)
            p = jnp.exp(scores - m[row])
            ssum = jax.ops.segment_sum(p, row, num_segments=L)
            alpha = p / ssum[row]
            out = jax.ops.segment_sum(alpha[:, :, None] * v[col], row, num_segments=L)
            return out.reshape(L, C) @ Wo + bo
        z = _ln(x, ln1_g, ln1_b)
        att = _sparse_attention(z, row_index, col_index, att_bias, Wq, bq, Wk, bk, Wv, bv, Wo, bo)
        x = x + att
        z = _ln(x, ln2_g, ln2_b)
        ff = jax.nn.silu(z @ W1 + b1) @ W2 + b2
        return x + ff

    def _L1_gnn_ref(x, edge_index, edge_type, basis1, att1, gate_w1, root1, bias1, basis2, att2, gate_w2, root2, bias2):
        import jax, jax.numpy as jnp
        import numpy as np
        NUM_RELATIONS = 2
        NUM_BASES = 30
        HIDDEN = 512
        N_NODES = 10000
        N_EDGES = 2500

        def rgcn_gate_layer(x, row, col, edge_type, basis, att, gate_w, root, bias):
            H = x.shape[1]
            w = jnp.einsum('rb,bio->rio', att, basis)
            x_j = x[col]
            msgs = []
            for r in range(NUM_RELATIONS):
                gate = jax.nn.sigmoid(x_j @ gate_w[r, :, 0])
                msgs.append(gate[:, None] * x_j @ w[r])
            msg = jnp.where((edge_type == 0)[:, None], msgs[0], msgs[1])
            agg = jax.ops.segment_sum(msg, row, num_segments=x.shape[0])
            return agg + x @ root + bias
        row, col = (edge_index[0], edge_index[1])
        h = jax.nn.relu(rgcn_gate_layer(x, row, col, edge_type, basis1, att1, gate_w1, root1, bias1))
        out = rgcn_gate_layer(h, row, col, edge_type, basis2, att2, gate_w2, root2, bias2)
        return out
    edge_index = jnp.stack([src, dst])
    x = _layernorm(x + _L0_gnn_ref(x, edge_attr_8, L0_gnn_Wq, L0_gnn_bq, L0_gnn_Wk, L0_gnn_bk, L0_gnn_Wv, L0_gnn_bv, L0_gnn_Wo, L0_gnn_bo, L0_gnn_ln1_g, L0_gnn_ln1_b, L0_gnn_ln2_g, L0_gnn_ln2_b, L0_gnn_W1, L0_gnn_b1, L0_gnn_W2, L0_gnn_b2, src, dst), axis=-1)
    x = _layernorm(x + _L1_gnn_ref(x, edge_index, edge_type_2, L1_gnn_basis1, L1_gnn_att1, L1_gnn_gate_w1, L1_gnn_root1, L1_gnn_bias1, L1_gnn_basis2, L1_gnn_att2, L1_gnn_gate_w2, L1_gnn_root2, L1_gnn_bias2), axis=-1)
    return x

_drawn_inputs = setup_inputs


def setup_inputs(seed=0):
    import zlib

    import numpy as np

    out = dict(_drawn_inputs(seed))
    spreads = {'L0_gnn_bq': (0.0, 0.8),
     'L0_gnn_bk': (0.0, 2.0),
     'L0_gnn_bv': (0.0, 0.342),
     'L0_gnn_bo': (0.0, 0.1),
     'L0_gnn_ln1_g': (1.0, 0.6),
     'L0_gnn_ln1_b': (0.0, 0.8),
     'L0_gnn_ln2_g': (1.0, 0.6),
     'L0_gnn_ln2_b': (0.0, 0.8),
     'L0_gnn_b1': (0.0, 0.46),
     'L0_gnn_b2': (0.0, 0.1)}
    factors = {'L0_gnn_Wq': 8.0,
     'L0_gnn_Wk': 8.0,
     'L1_gnn_basis1': 8.0,
     'L1_gnn_att1': 8.0,
     'L1_gnn_gate_w1': 8.0,
     'L1_gnn_root1': 8.0,
     'L1_gnn_bias1': 8.0,
     'L1_gnn_basis2': 8.0,
     'L1_gnn_att2': 8.0,
     'L1_gnn_gate_w2': 8.0,
     'L1_gnn_root2': 7.231,
     'L1_gnn_bias2': 8.0,
     'edge_attr_8': 3.88}
    for name, (base, spread) in spreads.items():
        noise = np.random.default_rng([zlib.crc32(name.encode()), seed]).standard_normal(out[name].shape)
        drawn = base * np.exp(spread * noise) if base else spread * noise
        out[name] = jnp.asarray(drawn.astype(out[name].dtype))
    for name, factor in factors.items():
        out[name] = (out[name] * factor).astype(out[name].dtype)
    return out
```

```python
from contextlib import ExitStack

import concourse.bass as bass
from concourse import mybir

F32, BF16, F16 = mybir.dt.float32, mybir.dt.bfloat16, mybir.dt.float16
I32, U32 = mybir.dt.int32, mybir.dt.uint32
ALU = mybir.AluOpType
ACT = mybir.ActivationFunctionType
AX = mybir.AxisListType.X
RMAX = bass.bass_isa.ReduceOp.max

P = 128
N = 512
C = 512
NC = C // P
H = 8
D = C // H
DV = D + 1
HID = 1024
NH = HID // P
EDGES = 16384
EC = EDGES // P
TYPES = 2
BASES = 30
EPS = 1e-5
SCALE = 1.0 / 8.0

BIN = 16
NBIN = N // BIN
NS = 160
FIELDS = 12
NM = H + TYPES
UW = 3 * H + TYPES
HI_W, LO_W = NM * BIN, H * BIN
RHS_W = UW * BIN

GROUPS = 4
BP = GROUPS * BASES
TILE_ROWS = 4
TILES = C // GROUPS // TILE_ROWS
RING = 3
NEG = -2.0 ** 100
TINY = 1e-37

COLS = ["L0_gnn_ln1_g", "L0_gnn_ln1_b", "L0_gnn_bq", "L0_gnn_bk", "L0_gnn_ln2_g", "L0_gnn_ln2_b", "L0_gnn_b1"]
ROWS = ["L0_gnn_bv", "L0_gnn_bo", "L0_gnn_b2", "L1_gnn_bias1", "L1_gnn_bias2"]


def span(start, end, step):
    return start, end - step + 1, step


def build(nc, x, src, dst, etype, attr, cols, rows, wq, wk, wv, wo, w1, w2, basis, att, gates, roots, out):
    edge_rows = nc.dram_tensor("edge_rows", (NS * P, FIELDS), F32).ap()
    w_rows = nc.dram_tensor("w_rows", (2, TYPES * GROUPS, P, C), F32).ap()

    ctx = ExitStack()
    with ctx:
        def sb(name, shape, dt=F32):
            return ctx.enter_context(nc.sbuf_tensor(name, shape, dt))

        def sem(name):
            return ctx.enter_context(nc.semaphore(name))

        dense = sb("dense", [P, NC * NM * N])
        mats = dense[:, :].rearrange("p (c a r) -> p c a r", c=NC, a=NM)
        qk = sb("qk", [P, 2 * H * N])
        q_t = qk[:, 0:H * N].rearrange("p (h n) -> p h n", h=H)
        k_t = qk[:, H * N:2 * H * N].rearrange("p (h n) -> p h n", h=H)
        v1 = sb("v1", [P, NC, H, DV])
        x0 = sb("x0", [P, NC, C])
        ring = sb("ring", [P, RING, TILE_ROWS * C])
        wrows = sb("wrows", [P, 2, 2, C])
        pool_mem = sb("pool_mem", [P, 7168])
        ident = sb("ident", [P, P])
        ident_b = sb("ident_b", [P, P], BF16)
        tri = sb("tri", [P, P])
        ones = sb("ones", [P, P])
        zero_blk = sb("att_blk", [P, 2, 32])
        iota_node = sb("iota_node", [P, N], F16)
        iota_bin = sb("iota_bin", [P, NBIN])
        iota_src = sb("iota_src", [P, BIN])
        iota_slot = sb("iota_slot", [1, NS])
        group_diff = sb("group_diff", [P, TYPES, GROUPS], I32)
        group_mask = sb("group_mask", [P, TYPES, GROUPS])
        att_sb = sb("att_sb", [BP, 2, TYPES])
        colv = sb("colv", [P, 4 * 6 + 8])
        bq_scaled = sb("bq_scaled", [P, NC])
        bv_row = sb("bv_row", [P, C])
        gate_w = sb("gate_w", [P, 2, NC, TYPES])
        stats = sb("stats", [P, NC, 6])
        mv = sb("mv", [P, NC, 2])
        rstd = sb("rstd", [P, NC])
        head_max = sb("head_max", [P, NC, H])
        head_neg = sb("head_neg", [P, NC, H])
        sums = sb("sums", [P, NC])
        gate = sb("gate", [P, NC, TYPES])
        slot_off = sb("slot_off", [1, NS], I32)
        bin_cum = sb("bin_cum", [P, NBIN + 1])
        bin_base = sb("bin_base", [P, NBIN + 1])
        bin_cnt = sb("bin_cnt", [P, NBIN])
        bin_slots_i = sb("bin_slots_i", [P, NBIN], I32)
        bin_slots_s = sb("bin_slots_s", [P, NBIN], I32)
        bin_slots = sb("bin_slots", [P, NBIN])
        bin_off = sb("bin_off", [P, NBIN])
        bias_max = sb("bias_max", [P, H])
        bias_top = sb("bias_top", [P, H])
        stage_idx = sb("stage_idx", [P, 2, 8], U32)
        stage_row = sb("stage_row", [P, 2, 8, FIELDS])
        ps = ctx.enter_context(nc.psum_tensor("ps", [P, 8, 512], F32))

        def carve(base, start, shape, dt=F32):
            n = 1
            for s in shape:
                n *= s
            size = n * (2 if dt in (BF16, F16) else 4) // 4
            v = base[:, start:start + size]
            v = v if dt == F32 else v.bitcast(dt)
            if len(shape) == 2:
                v = v.rearrange("p (a b) -> p a b", a=shape[0])
            elif len(shape) == 3:
                v = v.rearrange("p (a b c) -> p a b c", a=shape[0], b=shape[1])
            return v, start + size

        onehot_bin, at = carve(dense, 0, [NBIN, EC])
        running, at = carve(dense, at, [NBIN, EC])
        wqkv, at = carve(dense, at, [3, NC, C])
        z, at = carve(dense, at, [NC, C])
        z_t, at = carve(dense, at, [NC, N])
        src_i, at = carve(pool_mem, 0, [EC], I32)
        dst_i, at = carve(pool_mem, at, [EC], I32)
        typ_i, at = carve(pool_mem, at, [EC], I32)
        attr_sb, at = carve(pool_mem, at, [EC, H])
        fields, at = carve(pool_mem, at, [EC, FIELDS])
        src_lo, at = carve(pool_mem, at, [EC], I32)
        src_hi, at = carve(pool_mem, at, [EC], I32)
        bin_f, at = carve(pool_mem, at, [EC])
        pos, at = carve(pool_mem, at, [EC])
        pos_i, at = carve(pool_mem, at, [EC], I32)
        pos_lo, at = carve(pool_mem, at, [EC], I32)
        pos_hi, at = carve(pool_mem, at, [EC], I32)
        edge_idx, at = carve(pool_mem, at, [EC], U32)
        filler = pool_mem[:, at:at + NS * FIELDS].rearrange("p (s f) -> p s f", f=FIELDS)
        assert at + NS * FIELDS <= 7168
        edges, at = carve(pool_mem, 0, [NS, FIELDS])
        factors, at = carve(pool_mem, at, [NS, UW], BF16)
        in_bin, at = carve(pool_mem, at, [NS, BIN], BF16)
        targets, at_t = carve(pool_mem, at, [4, N], BF16)
        rhs, at_r = carve(pool_mem, at_t, [4, RHS_W], BF16)
        weight_f, _ = carve(pool_mem, at, [NS, H])
        assert at_r <= 7168 and at + NS * H <= 7168
        probs, at = carve(pool_mem, 0, [2, NC, N])
        none_t, none = probs[:, 0], probs[:, 1]
        none_tb = wrows[:, 0, :, :].rearrange("p a n -> p (a n)").bitcast(BF16).rearrange("p (c n) -> p c n", c=NC)
        exps, at = carve(pool_mem, at, [2, N])
        heads, at = carve(pool_mem, at, [NC, C])
        wo_sb = ring[:, 0, :].rearrange("p (c n) -> p c n", c=NC)
        w1_sb = ring[:, 1:3, :].rearrange("p a n -> p (a n)").rearrange("p (c n) -> p c n", c=NC)
        heads_t, x1 = q_t[:, 0:4], k_t[:, 0:4]
        z2_t, z2 = q_t[:, 4:8], k_t[:, 4:8]
        w2_sb, h1_t = mats[:, 0, 0:8], mats[:, 1, 0:8]
        row4, root_a = mats[:, 2, 0:4], mats[:, 2, 4:8]
        w_a = mats[:, 3, 0:8].rearrange("p (t c) n -> p t c n", t=TYPES)
        w_b = mats[:, 0, 0:8].rearrange("p (t c) n -> p t c n", t=TYPES)
        root_b = mats[:, 1, 0:4]
        msgs = probs
        y, y_t = q_t[:, 0:4], q_t[:, 4:8]
        g1_out, g1_t = k_t[:, 0:4], k_t[:, 4:8]

        edges_in, attr_in, x_in, small_in = sem("edges_in"), sem("attr_in"), sem("x_in"), sem("small_in")
        wqkv_in = sem("wqkv_in")
        consts = sem("consts")
        filled, fill_done = sem("filled"), sem("fill_done")
        dve_done = sem("dve_done")
        att_ready = sem("att_ready")
        basis_in = [sem(f"basis_in{i}") for i in range(RING)]
        basis_mm, basis_ev = sem("basis_mm"), sem("basis_ev")
        w_out = [sem(f"w_out{i}") for i in range(2)]
        pmax_ready, top_ready = sem("pmax_ready"), sem("top_ready")
        cnt_ready, cnt_mm, idx_ready = sem("cnt_ready"), sem("cnt_mm"), sem("idx_ready")
        staged, stage_go = sem("staged"), sem("stage_go")
        scattered = [sem(f"scattered{i}") for i in range(2)]
        sorted_in = sem("sorted_in")
        var_ready, std_ready = sem("var_ready"), sem("std_ready")
        z_ready, z_mm, z_ev = sem("z_ready"), sem("z_mm"), sem("z_ev")
        qk_mm, qk_ev, v_mm, v_ev = sem("qk_mm"), sem("qk_ev"), sem("v_mm"), sem("v_ev")
        w_exp, factor_ready = sem("w_exp"), sem("factor_ready")
        target_ready, rhs_ready, slot_mm, slot_added = sem("target_ready"), sem("rhs_ready"), sem("slot_mm"), sem("slot_added")
        none_b_ready = sem("none_b_ready")
        none_ready, none_mm, none_ev = sem("none_ready"), sem("none_mm"), sem("none_ev")
        max_mm, max_ev = sem("max_mm"), sem("max_ev")
        neg_ready, neg_mm, neg_ev = sem("neg_ready"), sem("neg_mm"), sem("neg_ev")
        st_mm, exp_done, prob_done, pv_mm, head_done = sem("st_mm"), sem("exp_done"), sem("prob_done"), sem("pv_mm"), sem("head_done")
        late_in, wo_in, w1_in, w2_in = sem("late_in"), sem("wo_in"), sem("w1_in"), sem("w2_in")
        wa_in, wb_in = sem("wa_in"), sem("wb_in")
        ht_mm, ht_ev, x1_mm = sem("ht_mm"), sem("ht_ev"), sem("x1_mm")
        z2_ready, z2_mm, z2_ev = sem("z2_ready"), sem("z2_mm"), sem("z2_ev")
        h1_mm, h1_ev, x2_mm = sem("h1_mm"), sem("h1_ev"), sem("x2_mm")
        y_ready, y_mm, y_ev = sem("y_ready"), sem("y_mm"), sem("y_ev")
        gate_mm, gate_ev = sem("gate_mm"), sem("gate_ev")
        msg_mm, msg_ev, agg_mm = sem("msg_mm"), sem("msg_ev"), sem("agg_mm")
        g1_ready, g1_mm, g1_ev = sem("g1_ready"), sem("g1_mm"), sem("g1_ev")
        out_ready, out_done = sem("out_ready"), sem("out_done")

        n_consts = 12
        block = ctx.enter_context(nc.Block())

        @block.sync
        def _(sp):
            sp.dma_start(src_i, src).then_inc(edges_in, 16)
            sp.dma_start(attr_sb, attr).then_inc(attr_in, 16)
            sp.dma_start(dst_i, dst).then_inc(edges_in, 16)
            sp.dma_start(typ_i, etype).then_inc(edges_in, 16)
            sp.dma_start(x0[:, :, :], x.rearrange("(c p) n -> p c n", p=P)).then_inc(x_in, 16)

            def basis_tile(layer, m, slot):
                rows_of = basis[layer].rearrange("b (g i) o -> (b g) (i o)", g=GROUPS)
                sp.dma_start(ring[0:BP, slot, :], rows_of[:, bass.ds(m * (TILE_ROWS * C), TILE_ROWS * C)])\
                  .then_inc(basis_in[slot], 16)

            for k in range(RING):
                basis_tile(0, k, k)
            for layer in range(2):
                first = RING if layer == 0 else 0
                at0 = layer * TILES
                lead = (-(at0 + first)) % RING
                turns = (TILES - first - lead) // RING
                for m in range(first, first + lead):
                    sp.wait_ge(basis_mm, at0 + m - RING + 1)
                    basis_tile(layer, m, (at0 + m) % RING)
                start = first + lead
                with sp.Fori(*span(start, start + turns * RING, RING)) as m:
                    for k in range(RING):
                        sp.wait_ge(basis_mm, m + (at0 + k - RING + 1))
                        basis_tile(layer, m + k, k)
                for m in range(start + turns * RING, TILES):
                    sp.wait_ge(basis_mm, at0 + m - RING + 1)
                    basis_tile(layer, m, (at0 + m) % RING)

            for i in range(2):
                sp.wait_ge(scattered[i], EC // 2 * 16)
            sp.wait_ge(fill_done, 16)
            sp.dma_start(edges, edge_rows.rearrange("(p s) f -> p s f", s=NS)).then_inc(sorted_in, 16)
            sp.wait_ge(basis_mm, 2 * TILES)
            sp.dma_start(wo_sb, wo.rearrange("(c p) n -> p c n", p=P)).then_inc(wo_in, 16)
            sp.dma_start(w1_sb, w1.rearrange("(c p) n -> p c n", p=P)).then_inc(w1_in, 16)
            sp.wait_ge(pv_mm, H)
            sp.dma_start(row4, rows[1:5, :].unsqueeze(0).to_broadcast([P, 4, C])).then_inc(late_in, 16)
            sp.dma_start(w2_sb, w2.rearrange("(c p) n -> p c n", p=P)).then_inc(w2_in, 16)
            for i in range(2):
                sp.wait_ge(w_out[i], 16 * 4 * (TILES // 2))
            sp.dma_start(w_a, w_rows[0].rearrange("(t c) p n -> p t c n", t=TYPES)).then_inc(wa_in, 16)
            sp.dma_start(root_a, roots[0].rearrange("(c p) n -> p c n", p=P)).then_inc(wa_in, 16)
            sp.wait_ge(x2_mm, NC)
            sp.dma_start(w_b, w_rows[1].rearrange("(t c) p n -> p t c n", t=TYPES)).then_inc(wb_in, 16)
            sp.dma_start(root_b, roots[1].rearrange("(c p) n -> p c n", p=P)).then_inc(wb_in, 16)
            for c in range(NC):
                sp.wait_ge(out_ready, c + 1)
                sp.dma_start(out[c * P:(c + 1) * P, :], g1_out[:, c, :]).then_inc(out_done, 16)
            sp.wait_ge(out_done, 16 * NC)

        @block.gpsimd
        def _(pool):
            pool.memset(filler, 0.0).then_inc(filled, 1)
            pool.wait_ge(filled, 1)
            pool.memset(filler[:, :, 1:2], -1.0).then_inc(filled, 1)
            pool.memset(filler[:, :, 4:FIELDS], -80.0).then_inc(filled, 1)
            pool.wait_ge(filled, 3)
            pool.dma_start(edge_rows.rearrange("(p s) f -> p s f", s=NS), filler).then_inc(fill_done, 16)
            pool.iota(iota_bin[:, :], [[1, NBIN]], base=0, channel_multiplier=0,
                      allow_small_or_imprecise_dtypes=True).then_inc(consts, 1)
            pool.iota(group_diff[:, :, :], [[0, TYPES], [-1, GROUPS]], base=0, channel_multiplier=1).then_inc(consts, 1)
            pool.memset(zero_blk[:, :, :], 0.0).then_inc(consts, 1)
            pool.memset(ones[:, :], 1.0).then_inc(consts, 1)
            pool.memset(ident[:, :], 0.0).then_inc(consts, 1)
            pool.wait_ge(consts, 5)
            pool.affine_select(out=tri[:, :], in_=ones[:, :], compare_op=ALU.is_gt, fill=0.0, base=0,
                               pattern=[[1, P]], channel_multiplier=-1).then_inc(consts, 1)
            pool.affine_select(out=ident[:, :], in_=ident[:, :], compare_op=ALU.not_equal, fill=1.0, base=0,
                               pattern=[[-1, P]], channel_multiplier=1).then_inc(consts, 1)
            pool.iota(iota_node[:, :], [[1, N]], base=0, channel_multiplier=0,
                      allow_small_or_imprecise_dtypes=True).then_inc(consts, 1)
            pool.iota(iota_src[:, :], [[1, BIN]], base=0, channel_multiplier=0,
                      allow_small_or_imprecise_dtypes=True).then_inc(consts, 1)
            pool.iota(iota_slot[:, :], [[1, NS]], base=0, channel_multiplier=0,
                      allow_small_or_imprecise_dtypes=True).then_inc(consts, 1)
            pool.wait_ge(consts, 10)
            pool.memset(k_t[64:65, :, :], 1.0).then_inc(consts, 1)
            pool.wait_ge(consts, 11)
            pool.memset(v1[:, :, :, D:DV], 1.0).then_inc(consts, 1)
            pool.wait_ge(pmax_ready, 1)
            pool.partition_all_reduce(bias_top[:, :], bias_max[:, :], P, RMAX).then_inc(top_ready, 1)

            pool.wait_ge(idx_ready, 1)
            pool.wait_ge(fill_done, 16)

            def scatter(j, half, turn, n):
                if turn is not None:
                    pool.wait_ge(scattered[half], turn)
                pool.tensor_copy(stage_idx[:, half, :], edge_idx[:, bass.ds(j, 8)]).then_inc(staged, 1)
                pool.tensor_copy(stage_row[:, half, :, :], fields[:, bass.ds(j, 8), :]).then_inc(staged, 1)
                pool.wait_ge(staged, n)
                pool.sem_inc(stage_go, 1)
                for k in range(8):
                    pool.indirect_dma_start(
                        out=edge_rows, out_offset=bass.IndirectOffsetOnAxis(ap=stage_idx[:, half, k:k + 1], axis=0),
                        in_=stage_row[:, half, k, :], in_offset=None).then_inc(scattered[half], 16)

            for half in range(2):
                scatter(8 * half, half, None, 2 * half + 2)
            with pool.Fori(*span(16, EC, 16)) as j:
                for half in range(2):
                    scatter(j + 8 * half, half, j * 8, j // 4 + (2 * half + 2))

            pool.wait_ge(factor_ready, 1)

            def slot_rhs(s, k, first):
                if not first:
                    pool.wait_ge(slot_mm, s - 3)
                pool.tensor_tensor(
                    rhs[:, k, :].rearrange("p (a r) -> p a r", r=BIN),
                    factors[:, bass.ds(s, 1), :].rearrange("p s a -> p (s a)").unsqueeze(2).to_broadcast([P, UW, BIN]),
                    in_bin[:, bass.ds(s, 1), :].to_broadcast([P, UW, BIN]), ALU.mult).then_inc(rhs_ready, 1)

            for k in range(4):
                slot_rhs(k, k, True)
            with pool.Fori(*span(4, NS, 4)) as s:
                for k in range(4):
                    slot_rhs(s + k, k, False)

        @block.scalar
        def _(act):
            act.dma_start(att_sb[:, :, :], att).then_inc(small_in, 16)
            act.dma_start(colv[:, :], cols).then_inc(small_in, 16)
            act.dma_start(gate_w[:, :, :, :], gates).then_inc(small_in, 16)
            act.dma_start(bv_row[:, :], rows[0:1, :].to_broadcast([P, C])).then_inc(small_in, 16)
            for i, w in enumerate((wq, wk, wv)):
                act.dma_start(wqkv[:, i], w.rearrange("(c p) n -> p c n", p=P)).then_inc(wqkv_in, 16)

            def root_of_variance(n):
                act.wait_ge(var_ready, n)
                act.activation(rstd[:, :], rstd[:, :], ACT.Sqrt).then_inc(std_ready, 1)

            def basis_rows(layer, m, half, n, turn):
                if turn is not None:
                    act.wait_ge(w_out[half], turn)
                for k in range(2):
                    act.wait_ge(basis_mm, n + (k + 1))
                    act.activation(wrows[:, half, k, :], ps[:, k, :], ACT.Copy).then_inc(basis_ev, 1)
                act.wait_ge(basis_ev, n + 2)
                to = w_rows[layer].rearrange("g (m j) o -> g m j o", j=TILE_ROWS)
                for j in range(TILE_ROWS):
                    act.dma_start(to[:, bass.ds(m, 2), j, :], wrows[32 * j:32 * j + TYPES * GROUPS, half, :, :])\
                       .then_inc(w_out[half], 16)

            def basis_layer(layer):
                at0 = layer * TILES
                start = 0
                if layer == 0:
                    for half in range(2):
                        basis_rows(0, 2 * half, half, 2 * half, None)
                    start = 4
                with act.Fori(*span(start, TILES, 4)) as m:
                    for half in range(2):
                        basis_rows(layer, m + 2 * half, half, m + (at0 + 2 * half), m * 16 + at0 * 16)

            basis_layer(0)
            root_of_variance(1)
            act.wait_ge(small_in, 64)
            for c in range(NC):
                act.wait_ge(z_mm, c + 1)
                act.activation(z_t[:, c, :], ps[:, 4 + c, :], ACT.Identity, scale=colv[:, c:c + 1],
                               bias=colv[:, 4 + c:5 + c]).then_inc(z_ev, 1)
            for g in range(2 * NC):
                kind, m = divmod(g, NC)
                act.wait_ge(qk_mm, g + 1)
                to = (q_t, k_t)[kind]
                for e in range(2):
                    bias = (bq_scaled[:, m:m + 1], colv[:, 12 + m:13 + m])[kind]
                    act.activation(to[0:D, 2 * m + e, :], ps[D * e:D * e + D, 4 + m, :], ACT.Identity,
                                   scale=(SCALE, 1.0)[kind], bias=bias[D * e:D * e + D]).then_inc(qk_ev, 1)
            basis_layer(1)

            act.wait_ge(sorted_in, 16)
            act.wait_ge(idx_ready, 1)
            act.activation(weight_f, edges[:, :, 4:FIELDS], ACT.Exp).then_inc(w_exp, 1)

            for c in range(NC):
                act.wait_ge(none_mm, c + 1)
                act.activation(none[:, c, :], ps[:, c, :], ACT.Copy).then_inc(none_ev, 1)
            for h in range(H):
                act.wait_ge(neg_mm, h + 1)
                act.activation(q_t[D:D + 1, h, :], ps[D:D + 1, h, :], ACT.Copy).then_inc(neg_ev, 1)
            for g in range(H * NC):
                act.wait_ge(st_mm, g + 1)
                if g >= 2:
                    act.wait_ge(prob_done, g - 1)
                act.activation(exps[:, g % 2, :], ps[:, g % 4, :], ACT.Exp).then_inc(exp_done, 1)
            for c in range(NC):
                act.wait_ge(ht_mm, c + 1)
                act.activation(heads_t[:, c, :], ps[:, c, :], ACT.Copy).then_inc(ht_ev, 1)
            root_of_variance(2)
            for c in range(NC):
                act.wait_ge(z2_mm, c + 1)
                act.activation(z2_t[:, c, :], ps[:, c, :], ACT.Identity, scale=colv[:, 16 + c:17 + c],
                               bias=colv[:, 20 + c:21 + c]).then_inc(z2_ev, 1)
            for m in range(NH):
                act.wait_ge(h1_mm, m + 1)
                act.activation(h1_t[:, m, :], ps[:, 4 + m % 4, :], ACT.Silu, bias=colv[:, 24 + m:25 + m]).then_inc(h1_ev, 1)
            root_of_variance(3)
            for c in range(NC):
                act.wait_ge(y_mm, c + 1)
                act.activation(y_t[:, c, :], ps[:, 4 + c, :], ACT.Copy).then_inc(y_ev, 1)
            for layer in range(2):
                act.wait_ge(gate_mm, layer + 1)
                act.activation(gate[:, :, :], ps[:, 0, 0:NC * TYPES].rearrange("p (c t) -> p c t", t=TYPES),
                               ACT.Sigmoid).then_inc(gate_ev, 1)
                act.wait_ge(gate_ev, layer + 1)
                for g in range(TYPES * NC):
                    t, c = divmod(g, NC)
                    act.wait_ge(msg_mm, TYPES * NC * layer + g + 1)
                    act.activation(msgs[:, t, c, :], ps[:, 4 + c, :], ACT.Copy,
                                   scale=gate[:, c, t:t + 1]).then_inc(msg_ev, 1)
                if layer == 0:
                    for c in range(NC):
                        act.wait_ge(g1_mm, c + 1)
                        act.activation(g1_t[:, c, :], ps[:, 4 + c, :], ACT.Relu).then_inc(g1_ev, 1)
            root_of_variance(4)

        @block.vector
        def _(dve):
            count = [0]

            def step(ins):
                count[0] += 1
                ins.then_inc(dve_done, 1)
                dve.wait_ge(dve_done, count[0])

            dve.wait_ge(consts, n_consts)
            step(dve.tensor_scalar(group_diff[:, :, :], group_diff[:, :, :], GROUPS - 1, None, ALU.bitwise_and))
            step(dve.tensor_scalar(group_mask[:, :, :], group_diff[:, :, :], 0.0, None, ALU.is_equal))
            dve.wait_ge(small_in, 64)
            for layer in range(2):
                dve.tensor_tensor(
                    zero_blk[0:BP, layer, 0:TYPES * GROUPS].rearrange("p (t g) -> p t g", t=TYPES), group_mask[0:BP, :, :],
                    att_sb[:, layer, :].unsqueeze(2).to_broadcast([BP, TYPES, GROUPS]), ALU.mult).then_inc(att_ready, 1)
            step(dve.tensor_copy(ident_b[:, :], ident[:, :]))
            step(dve.tensor_scalar(bq_scaled[:, :], colv[:, 8:12], SCALE, None, ALU.mult))

            dve.wait_ge(attr_in, 16)
            dve.tensor_reduce(bias_max[:, :], attr_sb.rearrange("p e h -> p h e"), AX, ALU.max).then_inc(pmax_ready, 1)

            dve.wait_ge(edges_in, 48)
            step(dve.tensor_scalar(src_hi, src_i, 4, None, ALU.logical_shift_right))
            step(dve.tensor_copy(bin_f, src_hi))
            step(dve.tensor_tensor(onehot_bin, bin_f.unsqueeze(1).to_broadcast([P, NBIN, EC]),
                                   iota_bin[:, :].unsqueeze(2).to_broadcast([P, NBIN, EC]), ALU.is_equal))
            flat_oh = onehot_bin.rearrange("p b e -> p (b e)")
            flat_run = running.rearrange("p b e -> p (b e)")
            step(dve.tensor_tensor_scan(flat_run, flat_oh, flat_oh, 0.0, ALU.add, ALU.max))
            step(dve.memset(bin_cum[:, 0:1], 0.0))
            step(dve.memset(bin_base[:, 0:1], 0.0))
            step(dve.tensor_copy(bin_cum[:, 1:NBIN + 1], running[:, :, EC - 1:EC].rearrange("p b e -> p (b e)")))
            dve.tensor_tensor(bin_cnt[:, :], bin_cum[:, 1:NBIN + 1], bin_cum[:, 0:NBIN], ALU.subtract).then_inc(cnt_ready, 1)
            dve.wait_ge(cnt_mm, 1)
            step(dve.tensor_scalar(bin_slots_i[:, :], ps[:, 2, NBIN:2 * NBIN], float(P - 1), None, ALU.add))
            step(dve.tensor_scalar(bin_slots_s[:, :], bin_slots_i[:, :], 7, None, ALU.logical_shift_right))
            step(dve.tensor_copy(bin_slots[:, :], bin_slots_s[:, :]))
            step(dve.tensor_tensor_scan(bin_base[:, 1:NBIN + 1], bin_slots[:, :], bin_slots[:, :], 0.0, ALU.add, ALU.max))
            step(dve.scalar_tensor_tensor(bin_off[:, :], bin_base[:, 0:NBIN], float(P), ps[:, 2, 0:NBIN], ALU.mult, ALU.add))
            step(dve.scalar_tensor_tensor(bin_off[:, :], bin_off[:, :], -1.0, bin_cum[:, 0:NBIN], ALU.add, ALU.subtract))
            step(dve.tensor_tensor(running, running, bin_off[:, :].unsqueeze(2).to_broadcast([P, NBIN, EC]), ALU.add))
            step(dve.tensor_tensor(running, running, onehot_bin, ALU.mult))
            step(dve.tensor_reduce(pos, running.rearrange("p b e -> p e b"), AX, ALU.add))
            step(dve.tensor_copy(pos_i, pos))
            step(dve.tensor_scalar(pos_lo, pos_i, P - 1, None, ALU.bitwise_and))
            step(dve.tensor_scalar(pos_hi, pos_i, 7, None, ALU.logical_shift_right))
            step(dve.scalar_tensor_tensor(edge_idx, pos_lo, float(NS), pos_hi, ALU.mult, ALU.add))
            step(dve.tensor_scalar(src_lo, src_i, BIN - 1, None, ALU.bitwise_and))
            for f, v in ((0, dst_i), (1, src_lo), (2, typ_i)):
                step(dve.tensor_copy(fields[:, :, f:f + 1].rearrange("p e f -> p (e f)"), v))
            step(dve.memset(fields[:, :, 3:4], 0.0))
            dve.wait_ge(top_ready, 1)
            dve.tensor_tensor(fields[:, :, 4:FIELDS], attr_sb, bias_top[:, :].unsqueeze(1).to_broadcast([P, EC, H]),
                              ALU.subtract).then_inc(idx_ready, 1)

            def norm(v, to, ready, n, parts=False):
                for c in range(NC):
                    step(dve.bn_stats(stats[:, c, :], v[:, c, :]))
                for c in range(NC):
                    step(dve.bn_aggr(mv[:, c, :], stats[:, c, :]))
                dve.tensor_scalar(rstd[:, :], mv[:, :, 1:2].rearrange("p c s -> p (c s)"), EPS, None, ALU.add)\
                   .then_inc(var_ready, 1)
                dve.wait_ge(std_ready, n)
                step(dve.reciprocal(rstd[:, :], rstd[:, :]))
                for c in range(NC):
                    dve.tensor_scalar(to[:, c, :], v[:, c, :], mv[:, c, 0:1], rstd[:, c:c + 1], ALU.subtract, ALU.mult)\
                       .then_inc(ready, 1)

            dve.wait_ge(x_in, 16)
            norm(x0, z, z_ready, 1)

            cmp = dense[0:1, 0:NS * NBIN].rearrange("p (s b) -> p s b", b=NBIN)
            step(dve.tensor_tensor(cmp, bin_base[0:1, 0:NBIN].unsqueeze(1).to_broadcast([1, NS, NBIN]),
                                   iota_slot[:, :].unsqueeze(2).to_broadcast([1, NS, NBIN]), ALU.is_le))
            slot_f = dense[0:1, NS * NBIN:NS * NBIN + NS]
            step(dve.tensor_reduce(slot_f, cmp, AX, ALU.add))
            step(dve.tensor_scalar(slot_off[:, :], slot_f, -1.0, float(BIN), ALU.add, ALU.mult))

            for c in range(NC):
                dve.wait_ge(v_mm, c + 1)
                dve.tensor_tensor(v1[:, c, :, 0:D], ps[:, 4 + c, :].rearrange("p (h d) -> p h d", h=H),
                                  bv_row[:, :].rearrange("p (h d) -> p h d", h=H), ALU.add).then_inc(v_ev, 1)

            step(dve.memset(dense[:, :], 0.0))

            dve.wait_ge(w_exp, 1)
            hi, mid, lo = (factors[:, :, a:a + H] for a in (0, H + TYPES, 2 * H + TYPES))
            step(dve.tensor_scalar(in_bin[:, :, :], edges[:, :, 1:2].to_broadcast([P, NS, BIN]), 0.0, None, ALU.add))
            step(dve.tensor_tensor(in_bin, in_bin, iota_src[:, :].unsqueeze(1).to_broadcast([P, NS, BIN]), ALU.is_equal))
            step(dve.tensor_scalar(factors[:, :, H:H + 1], edges[:, :, 2:3], 0.0, None, ALU.is_equal))
            step(dve.tensor_scalar(factors[:, :, H + 1:H + 2], edges[:, :, 2:3], 0.0, None, ALU.not_equal))
            step(dve.tensor_copy(hi, weight_f))
            step(dve.tensor_tensor(weight_f, weight_f, hi, ALU.subtract))
            step(dve.tensor_copy(mid, weight_f))
            step(dve.tensor_tensor(weight_f, weight_f, mid, ALU.subtract))
            dve.tensor_copy(lo, weight_f).then_inc(factor_ready, 1)
            dve.wait_ge(factor_ready, 1)

            def target(s, k):
                dve.tensor_scalar(targets[:, k, :], iota_node[:, :], edges[:, bass.ds(s, 1), 0:1].rearrange("p s f -> p (s f)"),
                                  None, ALU.is_equal).then_inc(target_ready, 1)

            def add_slot(s, k, first=False):
                offset = dve.value_load(slot_off[0:1, bass.ds(s, 1)], min_val=0, max_val=N - BIN)
                dve.wait_ge(slot_mm, s + 1)
                if not first:
                    dve.wait_ge(slot_added, s)
                to = mats.rearrange("p c a r -> p (c a) r")[:, :, bass.ds(offset, BIN)].rearrange("p (b a) r -> p b a r", b=2)
                got = ps[:, 2 * (k % 2):2 * (k % 2) + 2, 0:2 * HI_W].rearrange("p b (a r) -> p b a r", r=BIN)
                dve.tensor_tensor(to, got, to, ALU.add).then_inc(slot_added, 1)

            target(0, 0)
            target(1, 1)
            for k in range(4):
                target(k + 2, (k + 2) % 4)
                add_slot(k, k, first=k == 0)
            with dve.Fori(*span(4, NS - 4, 4)) as s:
                for k in range(4):
                    target(s + (k + 2), (k + 2) % 4)
                    add_slot(s + k, k)
            for k in range(4):
                if k < 2:
                    target(NS - 4 + k + 2, k + 2)
                add_slot(NS - 4 + k, k)
            dve.wait_ge(slot_added, NS)

            for i in range(2):
                dve.wait_ge(w_out[i], 16 * 4 * (TILES // 2))
            for c in range(NC):
                step(dve.tensor_tensor(none_t[:, c, :], mats[:, c, H, :], mats[:, c, H + 1, :], ALU.add))
                dve.tensor_scalar(none_t[:, c, :], none_t[:, c, :], 0.0, NEG, ALU.is_equal, ALU.mult).then_inc(none_ready, 1)
            dve.wait_ge(none_ready, NC)
            dve.tensor_copy(none_tb, none_t).then_inc(none_b_ready, 1)
            dve.wait_ge(none_ev, NC)
            for g in range(H * NC):
                h, c = divmod(g, NC)
                dve.wait_ge(max_mm, g + 1)
                dve.tensor_tensor_reduce(out=ps[:, 4 + c, :], in0=ps[:, 4 + c, :], in1=none[:, c, :], scale=1.0, scalar=NEG,
                                         op0=ALU.add, op1=ALU.max, accum_out=head_max[:, c, h:h + 1]).then_inc(max_ev, 1)
            dve.wait_ge(max_ev, H * NC)
            dve.tensor_scalar(head_neg[:, :, :], head_max[:, :, :], -1.0, None, ALU.mult).then_inc(neg_ready, 1)

            def head_out(h):
                o = ps[:, 4 + h % 2, 0:NC * DV].rearrange("p (c d) -> p c d", c=NC)
                dve.wait_ge(pv_mm, h + 1)
                step(dve.tensor_scalar(sums[:, :], o[:, :, D:DV].rearrange("p c d -> p (c d)"), TINY, None, ALU.max))
                step(dve.reciprocal(sums[:, :], sums[:, :]))
                dve.tensor_tensor(heads[:, :, h * D:(h + 1) * D], o[:, :, 0:D],
                                  sums[:, :].unsqueeze(2).to_broadcast([P, NC, D]), ALU.mult).then_inc(head_done, 1)

            for h in range(H):
                for c in range(NC):
                    dve.wait_ge(exp_done, NC * h + c + 1)
                    if h >= 2:
                        dve.wait_ge(pv_mm, h - 1)
                    dve.tensor_tensor(probs[:, h % 2, c, :], exps[:, c % 2, :], mats[:, c, h, :],
                                      ALU.mult).then_inc(prob_done, 1)
                if h >= 1:
                    head_out(h - 1)
                    dve.wait_ge(head_done, h)
            head_out(H - 1)

            dve.wait_ge(late_in, 16)
            for c in range(NC):
                dve.wait_ge(x1_mm, c + 1)
                step(dve.tensor_tensor(x1[:, c, :], ps[:, 4 + c, :], row4[:, 0, :], ALU.add))
                step(dve.tensor_tensor(x1[:, c, :], x1[:, c, :], x0[:, c, :], ALU.add))
            norm(x1, z2, z2_ready, 2)
            for c in range(NC):
                step(dve.tensor_tensor(x0[:, c, :], x0[:, c, :], x1[:, c, :], ALU.add))
                step(dve.tensor_tensor(x0[:, c, :], x0[:, c, :], row4[:, 1, :], ALU.add))
            for c in range(NC):
                dve.wait_ge(x2_mm, c + 1)
                step(dve.tensor_tensor(x0[:, c, :], ps[:, c, :], x0[:, c, :], ALU.add))
            norm(x0, y, y_ready, 3)
            for c in range(NC):
                dve.wait_ge(agg_mm, c + 1)
                dve.tensor_tensor(g1_out[:, c, :], ps[:, c, :], row4[:, 2, :], ALU.add).then_inc(g1_ready, 1)
            dve.wait_ge(y_ready, NC)
            for c in range(NC):
                step(dve.tensor_tensor(y[:, c, :], y[:, c, :], row4[:, 3, :], ALU.add))
            for c in range(NC):
                dve.wait_ge(agg_mm, NC + c + 1)
                step(dve.tensor_tensor(x0[:, c, :], ps[:, c, :], y[:, c, :], ALU.add))
            norm(x0, g1_out, out_ready, 4)

        @block.tensor
        def _(pe):
            mm = nc.tensor.matmul

            def transposes(v, bank, ready, done, per_chunk=True):
                pe.wait_ge(ready, NC)
                for c in range(NC):
                    for r in range(NC):
                        last = nc.tensor.transpose(ps[:, bank + c, r * P:(r + 1) * P], v[:, r, c * P:(c + 1) * P], ident[:, :])
                    last.then_inc(done, 1)

            def product(bank, pairs, done):
                for i, (l, r) in enumerate(pairs):
                    last = mm(ps[:, bank, :], l, r, start=i == 0, stop=i == len(pairs) - 1)
                last.then_inc(done, 1)

            def basis_tile(layer, m, slot, k, n, turn, free):
                pe.wait_ge(basis_in[slot], turn)
                if free is not None:
                    pe.wait_ge(basis_ev, free)
                for j in range(TILE_ROWS):
                    last = mm(ps[32 * j:32 * j + 32, k, :], zero_blk[0:BP, layer, :], ring[0:BP, slot, j * C:(j + 1) * C],
                              start=True, stop=True)
                last.then_inc(basis_mm, 1)

            def basis_layer(layer):
                at0 = layer * TILES
                pe.wait_ge(att_ready, layer + 1)
                turn = 2 * RING

                def written_out(m):
                    n = at0 + m
                    basis_tile(layer, m, n % RING, n % 2, n, 16 * (n // RING + 1), n - 1 if n >= 2 else None)

                lead = (-at0) % turn if at0 else turn
                turns = (TILES - lead) // turn
                for m in range(lead):
                    written_out(m)
                with pe.Fori(*span(lead, lead + turns * turn, turn)) as m:
                    for k in range(turn):
                        basis_tile(layer, m + k, k % RING, k % 2, None,
                                   (m + at0) * 16 // RING + 16 * (k // RING + 1), m + (at0 + k - 1))
                for m in range(lead + turns * turn, TILES):
                    written_out(m)

            pe.wait_ge(consts, n_consts)
            pe.wait_ge(cnt_ready, 1)
            mm(ps[:, 2, 0:NBIN], tri[:, :], bin_cnt[:, :], start=True, stop=True)
            mm(ps[:, 2, NBIN:2 * NBIN], ones[:, :], bin_cnt[:, :], start=True, stop=True).then_inc(cnt_mm, 1)
            basis_layer(0)
            transposes(z, 4, z_ready, z_mm)
            pe.wait_ge(wqkv_in, 48)
            pe.wait_ge(z_ev, NC)
            for g in range(2 * NC):
                kind, m = divmod(g, NC)
                if g >= NC:
                    pe.wait_ge(qk_ev, 2 * (g - NC + 1))
                product(4 + m, [(wqkv[:, kind, c, m * P:(m + 1) * P], z_t[:, c, :]) for c in range(NC)], qk_mm)
            for n in range(NC):
                pe.wait_ge(qk_ev, 2 * (NC + n + 1))
                product(4 + n, [(z_t[:, c, n * P:(n + 1) * P], wqkv[:, 2, c, :]) for c in range(NC)], v_mm)
            basis_layer(1)

            pe.wait_ge(basis_ev, 2 * TILES)

            def slot(s, k, first):
                pe.wait_ge(target_ready, s + 1)
                pe.wait_ge(rhs_ready, s + 1)
                if not first:
                    pe.wait_ge(slot_added, s - 1)
                for c in range(NC):
                    o = ps[:, 2 * (k % 2) + c // 2, HI_W * (c % 2):HI_W * (c % 2) + HI_W]
                    t = targets[:, k, c * P:(c + 1) * P]
                    mm(o, t, rhs[:, k, 0:HI_W], start=True, stop=False)
                    mm(o[:, 0:LO_W], t, rhs[:, k, HI_W:HI_W + LO_W], start=False, stop=False)
                    last = mm(o[:, 0:LO_W], t, rhs[:, k, HI_W + LO_W:RHS_W], start=False, stop=True)
                last.then_inc(slot_mm, 1)

            for k in range(4):
                slot(k, k, k < 2)
            with pe.Fori(*span(4, NS, 4)) as s:
                for k in range(4):
                    slot(s + k, k, False)

            pe.wait_ge(slot_added, NS)
            transposes(none_t, 0, none_ready, none_mm)
            for g in range(H * NC):
                h, c = divmod(g, NC)
                if g >= 4:
                    pe.wait_ge(max_ev, g - 3)
                product(4 + c, [(q_t[0:D, h, c * P:(c + 1) * P], k_t[0:D, h, :])], max_mm)
            pe.wait_ge(neg_ready, 1)
            for h in range(H):
                for c in range(NC):
                    last = mm(ps[D:D + 1, h, c * P:(c + 1) * P], head_neg[:, c, h:h + 1], ident[:, :], start=True, stop=True)
                last.then_inc(neg_mm, 1)

            def scores_t(h):
                for c in range(NC):
                    g = NC * h + c
                    if g >= 4:
                        pe.wait_ge(exp_done, g - 3)
                    mm(ps[:, g % 4, :], k_t[0:DV, h, c * P:(c + 1) * P], q_t[0:DV, h, :], start=True, stop=False)
                    mm(ps[:, g % 4, :], ident_b[:, :], none_tb[:, c, :], start=False, stop=True).then_inc(st_mm, 1)

            def values(h):
                pe.wait_ge(prob_done, NC * (h + 1))
                if h >= 2:
                    pe.wait_ge(head_done, h - 1)
                for r in range(NC):
                    for c in range(NC):
                        last = mm(ps[:, 4 + h % 2, r * DV:(r + 1) * DV], probs[:, h % 2, c, r * P:(r + 1) * P],
                                  v1[:, c, h, :], start=c == 0, stop=c == NC - 1)
                last.then_inc(pv_mm, 1)

            pe.wait_ge(neg_ev, H)
            pe.wait_ge(none_b_ready, 1)
            scores_t(0)
            for h in range(H):
                if h + 1 < H:
                    scores_t(h + 1)
                values(h)

            pe.wait_ge(head_done, H)
            for c in range(NC):
                for r in range(NC):
                    last = nc.tensor.transpose(ps[:, c, r * P:(r + 1) * P], heads[:, r, c * P:(c + 1) * P], ident[:, :])
                last.then_inc(ht_mm, 1)
            pe.wait_ge(wo_in, 16)
            pe.wait_ge(ht_ev, NC)
            for n in range(NC):
                product(4 + n, [(heads_t[:, c, n * P:(n + 1) * P], wo_sb[:, c, :]) for c in range(NC)], x1_mm)
            transposes(z2, 0, z2_ready, z2_mm)
            pe.wait_ge(w1_in, 16)
            pe.wait_ge(z2_ev, NC)
            for m in range(NH):
                if m >= 4:
                    pe.wait_ge(h1_ev, m - 3)
                product(4 + m % 4, [(w1_sb[:, c, m * P:(m + 1) * P], z2_t[:, c, :]) for c in range(NC)], h1_mm)
            pe.wait_ge(w2_in, 16)
            pe.wait_ge(h1_ev, NH)
            for n in range(NC):
                product(n, [(h1_t[:, m, n * P:(n + 1) * P], w2_sb[:, m, :]) for m in range(NH)], x2_mm)
            transposes(y, 4, y_ready, y_mm)
            for layer in range(2):
                in_t = (y_t, g1_t)[layer]
                root, w = ((root_a, w_a), (root_b, w_b))[layer]
                pe.wait_ge((y_ev, g1_ev)[layer], NC)
                if layer == 0:
                    pe.wait_ge(y_ready, NC)
                for n in range(NC):
                    for c in range(NC):
                        last = mm(ps[:, 0, n * TYPES:(n + 1) * TYPES], in_t[:, c, n * P:(n + 1) * P], gate_w[:, layer, c, :],
                                  start=c == 0, stop=c == NC - 1)
                last.then_inc(gate_mm, 1)
                pe.wait_ge((wa_in, wb_in)[layer], 32)
                for g in range(TYPES * NC):
                    t, n = divmod(g, NC)
                    if g >= 4:
                        pe.wait_ge(msg_ev, TYPES * NC * layer + g - 3)
                    product(4 + n, [(in_t[:, c, n * P:(n + 1) * P], w[:, t, c, :]) for c in range(NC)], msg_mm)
                pe.wait_ge(msg_ev, TYPES * NC * (layer + 1))
                for n in range(NC):
                    product(n, [(in_t[:, c, n * P:(n + 1) * P], root[:, c, :]) for c in range(NC)]
                            + [(mats[:, c, H + t, n * P:(n + 1) * P], msgs[:, t, c, :]) for t in range(TYPES) for c in range(NC)],
                            agg_mm)
                if layer == 0:
                    transposes(g1_out, 4, g1_ready, g1_mm)


def kernel(**inputs):
    import numpy as np
    import concourse.bacc as bacc
    from concourse.bass_utils import run_bass_kernel_spmd

    def a(name):
        return np.ascontiguousarray(np.asarray(inputs[name]))

    def column(v):
        return v.reshape(-1, P).T

    gates = np.stack([a(f"L1_gnn_gate_w{i}").reshape(TYPES, NC, P) for i in (1, 2)])
    att = np.stack([np.repeat(a(f"L1_gnn_att{i}").T, GROUPS, axis=0) for i in (1, 2)], axis=1)
    arrays = {
        "x": a("x"), "src": a("src").reshape(P, EC), "dst": a("dst").reshape(P, EC),
        "etype": a("edge_type_2").reshape(P, EC), "attr": a("edge_attr_8").reshape(P, EC, H),
        "cols": np.concatenate([column(a(n)) for n in COLS], axis=1),
        "rows": np.stack([a(n) for n in ROWS]),
        "wq": a("L0_gnn_Wq"), "wk": a("L0_gnn_Wk"), "wv": a("L0_gnn_Wv"), "wo": a("L0_gnn_Wo"),
        "w1": a("L0_gnn_W1"), "w2": a("L0_gnn_W2"),
        "basis1": a("L1_gnn_basis1"), "basis2": a("L1_gnn_basis2"), "att": att,
        "gates": gates.transpose(3, 0, 2, 1), "root1": a("L1_gnn_root1"), "root2": a("L1_gnn_root2"),
    }
    arrays = {k: np.ascontiguousarray(v) for k, v in arrays.items()}
    nc = bacc.Bacc("TRN2", target_bir_lowering=False, num_devices=1)
    t = {k: nc.dram_tensor(k, v.shape, mybir.dt.from_np(v.dtype), kind="ExternalInput").ap() for k, v in arrays.items()}
    out = nc.dram_tensor("out", (N, C), F32, kind="ExternalOutput").ap()
    build(nc, t["x"], t["src"], t["dst"], t["etype"], t["attr"], t["cols"], t["rows"], t["wq"], t["wk"], t["wv"],
          t["wo"], t["w1"], t["w2"], [t["basis1"], t["basis2"]], t["att"], t["gates"], [t["root1"], t["root2"]], out)
    r = run_bass_kernel_spmd(nc, [arrays], core_ids=[0])
    return r.results[0]["out"]
```

```python
from contextlib import ExitStack

import concourse.bass as bass
from concourse import mybir

F32, BF16, F16 = mybir.dt.float32, mybir.dt.bfloat16, mybir.dt.float16
I32, U32 = mybir.dt.int32, mybir.dt.uint32
ALU = mybir.AluOpType
ACT = mybir.ActivationFunctionType
AX = mybir.AxisListType.X
RMAX = bass.bass_isa.ReduceOp.max

P = 128
N = 512
C = 512
NC = C // P
H = 8
D = C // H
SLOT_TURN = 16
TILED = 128
HID = 1024
NH = HID // P
EDGES = 16384
EC = EDGES // P
TYPES = 2
BASES = 30
EPS = 1e-5
SCALE = 1.0 / 8.0

BIN = 16
NBIN = N // BIN
NS = 160
FIELDS = 12
NM = H + TYPES
UW = 3 * H + TYPES
HI_W, LO_W = NM * BIN, H * BIN
RHS_W = UW * BIN

GROUPS = 4
BP = GROUPS * BASES
TILE_ROWS = 4
TILES = C // GROUPS // TILE_ROWS
RING = 4
NO_EDGE = 2.0 ** 100
TINY = 1e-37
STEPS = H * NC
EXP_LAG, VALUE_LAG = 5, 7
ADDED0, MM0, TILE0, EV0 = 2, 4, RING, 2

COLS = ["L0_gnn_ln1_g", "L0_gnn_ln1_b", "L0_gnn_bq", "L0_gnn_bk", "L0_gnn_ln2_g", "L0_gnn_ln2_b", "L0_gnn_b1"]
ROWS = ["L0_gnn_bv", "L0_gnn_bo", "L0_gnn_b2", "L1_gnn_bias1", "L1_gnn_bias2"]


def span(start, end, step):
    return start, end - step + 1, step


def build(nc, x, src, dst, etype, attr, cols, rows, wq, wk, wv, wo, w1, w2, basis, att, gates, roots, out):
    edge_rows = nc.dram_tensor("edge_rows", (NS * P, FIELDS), F32).ap()
    w_rows = nc.dram_tensor("w_rows", (2, TYPES * GROUPS, P, C), F32).ap()

    ctx = ExitStack()
    with ctx:
        def sb(name, shape, dt=F32):
            return ctx.enter_context(nc.sbuf_tensor(name, shape, dt))

        def sem(name):
            return ctx.enter_context(nc.semaphore(name))

        dense = sb("dense", [P, NC * NM * N])
        mats = dense[:, :].rearrange("p (c a r) -> p c a r", c=NC, a=NM)
        qk = sb("qk", [P, 2 * H * N])
        q_t = qk[:, 0:H * N].rearrange("p (h n) -> p h n", h=H)
        k_t, heads_t = (qk[:, a * N:(a + NC) * N].rearrange("p (c n) -> p c n", c=NC) for a in (H, H + NC))
        v1 = sb("v1", [P, NC, H // 2, 3, D])
        x0 = sb("x0", [P, NC, C])
        ring = sb("ring", [P, RING, TILE_ROWS * C])
        wrows = sb("wrows", [P, 2, 2, C])
        pool_mem = sb("pool_mem", [P, 7200])
        stage_idx = sb("stage_idx", [P, 2, 8], U32)
        stage_row = sb("stage_row", [P, 2, 8, FIELDS])
        ident = sb("ident", [P, P])
        ident_b = sb("ident_b", [P, P], BF16)
        tri = sb("tri", [P, P])
        ones = sb("ones", [P, P])
        zero_blk = sb("att_blk", [P, 2, 32])
        iota_node = sb("iota_node", [P, N], F16)
        iota_bin = sb("iota_bin", [P, NBIN])
        iota_src = sb("iota_src", [P, BIN])
        iota_slot = sb("iota_slot", [1, NS])
        group_diff = sb("group_diff", [P, TYPES, GROUPS], I32)
        group_mask = sb("group_mask", [P, TYPES, GROUPS])
        att_sb = sb("att_sb", [BP, 2, TYPES])
        colv = sb("colv", [P, 4 * 6 + 8])
        bq_scaled = sb("bq_scaled", [P, NC])
        stats = sb("stats", [P, NC, 6])
        mv = sb("mv", [P, NC, 2])
        rstd = sb("rstd", [P, NC])
        neg_max = sb("neg_max", [P, H, NC])
        gate_dot = sb("gate_dot", [P, NC, TYPES])
        gate = sb("gate", [P, NC, TYPES])
        slot_off = sb("slot_off", [1, NS], I32)
        ps = ctx.enter_context(nc.psum_tensor("ps", [P, 8, 512], F32))

        def carve(base, start, shape, dt=F32):
            n = 1
            for s in shape:
                n *= s
            size = n * (2 if dt in (BF16, F16) else 4) // 4
            v = base[:, start:start + size]
            v = v if dt == F32 else v.bitcast(dt)
            if len(shape) == 2:
                v = v.rearrange("p (a b) -> p a b", a=shape[0])
            elif len(shape) == 3:
                v = v.rearrange("p (a b c) -> p a b c", a=shape[0], b=shape[1])
            return v, start + size

        onehot_bin, at = carve(dense, 0, [NBIN, EC])
        running, at = carve(dense, at, [NBIN, EC])
        wqkv, at = carve(dense, at, [3, NC, C])
        z, at = carve(dense, at, [NC, C])
        z_t, at = carve(dense, at, [NC, N])
        bv_row = dense[:, at:at + C]
        src_i, at = carve(pool_mem, 0, [EC], I32)
        dst_i, at = carve(pool_mem, at, [EC], I32)
        typ_i, at = carve(pool_mem, at, [EC], I32)
        attr_sb, at = carve(pool_mem, at, [EC, H])
        fields, at = carve(pool_mem, at, [EC, FIELDS])
        src_lo, at = carve(pool_mem, at, [EC], I32)
        src_hi, at = carve(pool_mem, at, [EC], I32)
        bin_f, at = carve(pool_mem, at, [EC])
        pos, at = carve(pool_mem, at, [EC])
        pos_i, at = carve(pool_mem, at, [EC], I32)
        pos_lo, at = carve(pool_mem, at, [EC], I32)
        pos_hi, at = carve(pool_mem, at, [EC], I32)
        edge_idx, at = carve(pool_mem, at, [EC], U32)
        filler = pool_mem[:, at:at + NS * FIELDS].rearrange("p (s f) -> p s f", f=FIELDS)
        assert at + NS * FIELDS <= 7200
        sort_mem = wrows[:, :, :, :].rearrange("p a b n -> p (a b n)")
        bin_cum, at = sort_mem[:, 0:NBIN + 1], NBIN + 1
        bin_base, at = sort_mem[:, at:at + NBIN + 1], at + NBIN + 1
        bin_cnt, at = carve(sort_mem, at, [NBIN])
        bin_slots_i, at = carve(sort_mem, at, [NBIN], I32)
        bin_slots_s, at = carve(sort_mem, at, [NBIN], I32)
        bin_slots, at = carve(sort_mem, at, [NBIN])
        bin_off, at = carve(sort_mem, at, [NBIN])
        bias_max, at = carve(sort_mem, at, [H])
        bias_top, at = carve(sort_mem, at, [H])
        edges, at = carve(pool_mem, 0, [NS + 2, FIELDS])
        factors, at = carve(pool_mem, at, [NS, UW], BF16)
        in_bin, at = carve(pool_mem, at, [NS, BIN], BF16)
        targets, at_t = carve(pool_mem, at, [4, N], BF16)
        rhs, at_r = carve(pool_mem, at_t, [4, RHS_W], BF16)
        weight_f, _ = carve(pool_mem, at, [NS, H])
        assert at_r <= 7200 and at + NS * H <= 7200
        exps, at = carve(pool_mem, 0, [2, NC, N])
        probs, at = carve(pool_mem, at, [NC, N])
        inv_sum, at = carve(pool_mem, at, [N])
        none_t, none = probs, ring[:, 3, :].rearrange("p (c n) -> p c n", c=NC)
        row4 = wrows[:, :, :, :].rearrange("p a b n -> p (a b) n")
        wo_sb = ring[:, 0, :].rearrange("p (c n) -> p c n", c=NC)
        w1_sb = ring[:, 1:3, :].rearrange("p a n -> p (a n)").rearrange("p (c n) -> p c n", c=NC)
        w2_sb, root_a, w_a = mats[:, :, 0:2], mats[:, :, 2], mats[:, :, 3:5]
        w_b, root_b = mats[:, :, 5:7], mats[:, :, 7]
        z2, z2_t, x1 = q_t[:, 0:4], q_t[:, 4:8], k_t
        h1_t = exps[:, :, :, :].rearrange("p a c n -> p (a c) n")
        msgs, (junk, at) = exps, carve(pool_mem, H * N, [2, N])
        gate_rows, at = carve(pool_mem, at, [2 * TYPES, C])
        y, y_t, g1_out, g1_t = z2, z2_t, x1, heads_t
        assert at <= 7200

        edges_in, attr_in, x_in, small_in = sem("edges_in"), sem("attr_in"), sem("x_in"), sem("small_in")
        wqkv_in = sem("wqkv_in")
        consts, bin_const = sem("consts"), sem("bin_const")
        filled, fill_done = sem("filled"), sem("fill_done")
        dve_done = sem("dve_done")
        att_ready = sem("att_ready")
        basis_in = [sem(f"basis_in{i}") for i in range(RING)]
        basis_mm, basis_ev = sem("basis_mm"), sem("basis_ev")
        w_out = [sem(f"w_out{i}") for i in range(2)]
        pmax_ready, top_ready = sem("pmax_ready"), sem("top_ready")
        bins_read, bq_ready = sem("bins_read"), sem("bq_ready")
        cnt_ready, cnt_mm, idx_ready = sem("cnt_ready"), sem("cnt_mm"), sem("idx_ready")
        staged, stage_go = sem("staged"), sem("stage_go")
        scattered = [sem(f"scattered{i}") for i in range(2)]
        sorted_in = sem("sorted_in")
        var_ready, std_ready = sem("var_ready"), sem("std_ready")
        z_ready, z_mm, z_ev = sem("z_ready"), sem("z_mm"), sem("z_ev")
        qk_mm, qk_ev, v_mm, v_ev = sem("qk_mm"), sem("qk_ev"), sem("v_mm"), sem("v_ev")
        w_exp, factor_ready = sem("w_exp"), sem("factor_ready")
        target_ready = sem("target_ready")
        rhs_ready, slot_mm, slot_added = sem("rhs_ready"), sem("slot_mm"), sem("slot_added")
        none_ready, none_mm, none_ev = sem("none_ready"), sem("none_mm"), sem("none_ev")
        score_mm, max_ready, exp_done = sem("score_mm"), sem("max_ready"), sem("exp_done")
        exp_mm, prob_done, value_mm, head_done = (sem(n) for n in (
            "exp_mm", "prob_done", "value_mm", "head_done"))
        late_in, wo_in, w1_in, w2_in = sem("late_in"), sem("wo_in"), sem("w1_in"), sem("w2_in")
        wa_in, wb_in = sem("wa_in"), sem("wb_in")
        x1_mm, gates_in = sem("x1_mm"), sem("gates_in")
        z2_ready, z2_mm, z2_ev = sem("z2_ready"), sem("z2_mm"), sem("z2_ev")
        h1_mm, h1_ev, x2_mm = sem("h1_mm"), sem("h1_ev"), sem("x2_mm")
        y_ready, y_mm, y_ev = sem("y_ready"), sem("y_mm"), sem("y_ev")
        gate_ready, gate_ev = sem("gate_ready"), sem("gate_ev")
        msg_mm, msg_ev, agg_mm = sem("msg_mm"), sem("msg_ev"), sem("agg_mm")
        g1_ready, g1_mm, g1_ev = sem("g1_ready"), sem("g1_mm"), sem("g1_ev")
        out_ready, out_done = sem("out_ready"), sem("out_done")

        n_consts = 11
        block = ctx.enter_context(nc.Block())

        @block.sync
        def _(sp):
            sp.dma_start(src_i, src).then_inc(edges_in, 16)
            sp.dma_start(attr_sb, attr).then_inc(attr_in, 16)
            sp.dma_start(dst_i, dst).then_inc(edges_in, 16)
            sp.dma_start(typ_i, etype).then_inc(edges_in, 16)

            for layer in range(2):
                rows_of = basis[layer].rearrange("b (g i) o -> (b g) (i o)", g=GROUPS)
                to = w_rows[layer].rearrange("g (m j) o -> g m j o", j=TILE_ROWS)

                def load_tiles(m):
                    for k in range(RING):
                        sp.wait_ge(basis_mm, m + (layer * TILES + k + 1))
                        sp.dma_start(ring[0:BP, k, :], rows_of[:, bass.ds((m + k) * (TILE_ROWS * C), TILE_ROWS * C)])\
                          .then_inc(basis_in[k], 16)

                def store_rows(m):
                    for half in range(2):
                        sp.wait_ge(basis_ev, m + (layer * TILES + 2 * half + 2 + EV0))
                        for j in range(TILE_ROWS):
                            sp.dma_start(to[:, bass.ds(m + 2 * half, 2), j, :],
                                         wrows[32 * j:32 * j + TYPES * GROUPS, half, :, :]).then_inc(w_out[half], 16)

                load_tiles(0)
                with sp.Fori(*span(RING, TILES, RING)) as m:
                    load_tiles(m)
                    store_rows(m - RING)
                store_rows(TILES - RING)

            sp.wait_ge(basis_mm, 2 * TILES + TILE0)
            sp.dma_start(wo_sb, wo.rearrange("(c p) n -> p c n", p=P)).then_inc(wo_in, 16)
            sp.dma_start(w1_sb, w1.rearrange("(c p) n -> p c n", p=P)).then_inc(w1_in, 16)
            for i in range(2):
                sp.wait_ge(w_out[i], 16 * 4 * (TILES // 2))
            sp.dma_start(row4, rows[1:5, :].unsqueeze(0).to_broadcast([P, 4, C])).then_inc(late_in, 16)
            sp.wait_ge(prob_done, 2 * NC)
            for c in range(NC):
                sp.dma_start(w2_sb[:, c], w2[2 * P * c:2 * P * (c + 1), :].rearrange("(k p) n -> p k n", p=P)).then_inc(w2_in, 16)
            for layer, (w_to, root_to, w_done) in enumerate(((w_a, root_a, wa_in), (w_b, root_b, wb_in))):
                sp.wait_ge(prob_done, (5, 8)[layer] * NC)
                for c in range(NC):
                    sp.dma_start(w_to[:, c], w_rows[layer].rearrange("(t c) p n -> p c t n", t=TYPES)[:, c]).then_inc(w_done, 16)
                sp.dma_start(root_to, roots[layer].rearrange("(c p) n -> p c n", p=P)).then_inc(w_done, 16)
            sp.wait_ge(head_done, H)
            sp.dma_start(gate_rows, gates.unsqueeze(0).to_broadcast([P, 2 * TYPES, C])).then_inc(gates_in, 16)
            for c in range(NC):
                sp.wait_ge(out_ready, c + 1)
                sp.dma_start(out[c * P:(c + 1) * P, :], g1_out[:, c, :]).then_inc(out_done, 16)
            sp.wait_ge(out_done, 16 * NC)

        @block.gpsimd
        def _(pool):
            pool.iota(iota_bin[:, :], [[1, NBIN]], base=0, channel_multiplier=0,
                      allow_small_or_imprecise_dtypes=True).then_inc(bin_const, 1)
            pool.memset(ones[:, :], 1.0).then_inc(consts, 1)
            pool.memset(ident[:, :], 0.0).then_inc(consts, 1)
            pool.wait_ge(consts, 2)
            pool.affine_select(out=tri[:, :], in_=ones[:, :], compare_op=ALU.is_gt, fill=0.0, base=0,
                               pattern=[[1, P]], channel_multiplier=-1).then_inc(consts, 1)
            pool.affine_select(out=ident[:, :], in_=ident[:, :], compare_op=ALU.not_equal, fill=1.0, base=0,
                               pattern=[[-1, P]], channel_multiplier=1).then_inc(consts, 1)
            pool.memset(filler, 0.0).then_inc(filled, 1)
            pool.wait_ge(filled, 1)
            pool.memset(filler[:, :, 1:2], -1.0).then_inc(filled, 1)
            pool.memset(filler[:, :, 4:FIELDS], -80.0).then_inc(filled, 1)
            pool.wait_ge(filled, 3)
            pool.dma_start(edge_rows.rearrange("(p s) f -> p s f", s=NS), filler).then_inc(fill_done, 16)
            pool.iota(iota_node[:, :], [[1, N]], base=0, channel_multiplier=0,
                      allow_small_or_imprecise_dtypes=True).then_inc(consts, 1)
            pool.iota(iota_src[:, :], [[1, BIN]], base=0, channel_multiplier=0,
                      allow_small_or_imprecise_dtypes=True).then_inc(consts, 1)
            pool.iota(iota_slot[:, :], [[1, NS]], base=0, channel_multiplier=0,
                      allow_small_or_imprecise_dtypes=True).then_inc(consts, 1)
            pool.iota(group_diff[:, :, :], [[0, TYPES], [-1, GROUPS]], base=0, channel_multiplier=1).then_inc(consts, 1)
            pool.memset(zero_blk[:, :, :], 0.0).then_inc(consts, 1)
            pool.memset(q_t, 0.0).then_inc(consts, 1)
            pool.memset(v1[:, :, :, 1, :], 1.0).then_inc(consts, 1)
            pool.wait_ge(pmax_ready, 1)
            pool.partition_all_reduce(bias_top[:, :], bias_max[:, :], P, RMAX).then_inc(top_ready, 1)

            pool.wait_ge(idx_ready, 1)
            pool.wait_ge(fill_done, 16)

            def scatter(j, half, turn, n):
                if turn is not None:
                    pool.wait_ge(scattered[half], turn)
                pool.tensor_copy(stage_idx[:, half, :], edge_idx[:, bass.ds(j, 8)]).then_inc(staged, 1)
                pool.tensor_copy(stage_row[:, half, :, :], fields[:, bass.ds(j, 8), :]).then_inc(staged, 1)
                pool.wait_ge(staged, n)
                pool.sem_inc(stage_go, 1)
                for k in range(8):
                    pool.indirect_dma_start(
                        out=edge_rows, out_offset=bass.IndirectOffsetOnAxis(ap=stage_idx[:, half, k:k + 1], axis=0),
                        in_=stage_row[:, half, k, :], in_offset=None).then_inc(scattered[half], 16)

            for half in range(2):
                scatter(8 * half, half, None, 2 * half + 2)
            with pool.Fori(*span(16, EC, 16)) as j:
                for half in range(2):
                    scatter(j + 8 * half, half, j * 8, j // 4 + (2 * half + 2))

            for i in range(2):
                pool.wait_ge(scattered[i], EC // 2 * 16)
            pool.dma_start(edges[:, 0:NS, :], edge_rows.rearrange("(p s) f -> p s f", s=NS)).then_inc(sorted_in, 16)

            pool.wait_ge(factor_ready, 1)
            with pool.Fori(*span(0, NS, 4)) as s:
                for k in range(4):
                    pool.wait_ge(slot_mm, s + (k + 1))
                    pool.tensor_tensor(
                        rhs[:, k, :].rearrange("p (a r) -> p a r", r=BIN),
                        factors[:, bass.ds(s + k, 1), :].rearrange("p s a -> p (s a)").unsqueeze(2).to_broadcast([P, UW, BIN]),
                        in_bin[:, bass.ds(s + k, 1), :].to_broadcast([P, UW, BIN]), ALU.mult).then_inc(rhs_ready, 1)

        @block.scalar
        def _(act):
            act.dma_start(x0[:, :, :], x.rearrange("(c p) n -> p c n", p=P)).then_inc(x_in, 16)
            act.dma_start(att_sb[:, :, :], att).then_inc(small_in, 16)
            act.dma_start(colv[:, :], cols).then_inc(small_in, 16)
            act.dma_start(bv_row, rows[0:1, :].to_broadcast([P, C])).then_inc(small_in, 16)
            for i, w in enumerate((wq, wk, wv)):
                act.dma_start(wqkv[:, i], w.rearrange("(c p) n -> p c n", p=P)).then_inc(wqkv_in, 16)
            act.sem_inc(basis_ev, EV0)

            def roots_of_variance(n):
                for c in range(NC):
                    act.wait_ge(var_ready, NC * n + c + 1)
                    act.activation(rstd[:, c:c + 1], rstd[:, c:c + 1], ACT.Sqrt).then_inc(std_ready, 1)

            def basis_rows(half, n, turn):
                if turn is not None:
                    act.wait_ge(w_out[half], turn)
                for k in range(2):
                    act.wait_ge(basis_mm, n + (k + 1 + TILE0))
                    act.activation(wrows[:, half, k, :], ps[:, 4 + k, :], ACT.Copy).then_inc(basis_ev, 1)

            roots_of_variance(0)
            act.wait_ge(small_in, 48)
            act.wait_ge(z_mm, NC)
            for c in range(NC):
                act.activation(z_t[:, c, :], ps[:, c, :], ACT.Identity, scale=colv[:, c:c + 1],
                               bias=colv[:, 4 + c:5 + c]).then_inc(z_ev, 1)
            act.wait_ge(bq_ready, 1)
            act.wait_ge(consts, n_consts)
            for g in range(2 * NC):
                kind, m = divmod(g, NC)
                act.wait_ge(qk_mm, g + 1)
                if kind == 0:
                    for e in range(2):
                        own = slice(D * e, D * e + D)
                        act.activation(q_t[own, 2 * m + e, :], ps[own, 4 + m, :], ACT.Identity, scale=-SCALE,
                                       bias=bq_scaled[own, m:m + 1]).then_inc(qk_ev, 1)
                else:
                    act.activation(k_t[:, m, :], ps[:, m, :], ACT.Identity, bias=colv[:, 12 + m:13 + m]).then_inc(qk_ev, 1)
            for half in range(2):
                basis_rows(half, 2 * half, None)
            with act.Fori(*span(4, TILES, 4)) as m:
                for half in range(2):
                    basis_rows(half, m + 2 * half, m * 16)

            act.wait_ge(sorted_in, 16)
            act.activation(weight_f, edges[:, 0:NS, 4:FIELDS], ACT.Exp).then_inc(w_exp, 1)

            with act.Fori(*span(0, TILES, 4)) as m:
                for half in range(2):
                    basis_rows(half, m + (TILES + 2 * half), m * 16 + TILES * 16)

            for c in range(NC):
                act.wait_ge(none_mm, NC)
                act.activation(none[:, c, :], ps[:, c, :], ACT.Copy).then_inc(none_ev, 1)
            for k in range(STEPS):
                h, r = divmod(k, NC)
                act.wait_ge(max_ready, k + 1)
                if h >= 2:
                    act.wait_ge(exp_mm, NC * (h - 1))
                act.activation(exps[:, h % 2, r, :], ps[:, r, :], ACT.Exp, scale=-1.0,
                               bias=neg_max[:, h, r:r + 1]).then_inc(exp_done, 1)
            roots_of_variance(1)
            act.wait_ge(z2_mm, NC)
            for c in range(NC):
                act.activation(z2_t[:, c, :], ps[:, c, :], ACT.Identity, scale=colv[:, 16 + c:17 + c],
                               bias=colv[:, 20 + c:21 + c]).then_inc(z2_ev, 1)
            for m in range(NH):
                act.wait_ge(h1_mm, m + 1)
                act.activation(h1_t[:, m, :], ps[:, 4 + m % 4, :], ACT.Silu, bias=colv[:, 24 + m:25 + m]).then_inc(h1_ev, 1)
            roots_of_variance(2)
            for layer in range(2):
                to, done, ev = ((y_t, y_mm, y_ev), (g1_t, g1_mm, g1_ev))[layer]
                act.wait_ge(done, NC)
                for c in range(NC):
                    act.activation(to[:, c, :], ps[:, 4 + c, :], ACT.Copy).then_inc(ev, 1)
                act.wait_ge(gate_ready, layer + 1)
                act.activation(gate[:, :, :], gate_dot[:, :, :], ACT.Sigmoid).then_inc(gate_ev, 1)
                act.wait_ge(gate_ev, layer + 1)
                for g in range(TYPES * NC):
                    t, c = divmod(g, NC)
                    act.wait_ge(msg_mm, TYPES * NC * layer + g + 1)
                    act.activation(msgs[:, t, c, :], ps[:, 4 + c, :], ACT.Copy,
                                   scale=gate[:, c, t:t + 1]).then_inc(msg_ev, 1)
            roots_of_variance(3)

        @block.vector
        def _(dve):
            count = [0]

            def step(ins):
                count[0] += 1
                ins.then_inc(dve_done, 1)
                dve.wait_ge(dve_done, count[0])

            dve.wait_ge(edges_in, 48)
            dve.wait_ge(bin_const, 1)
            step(dve.tensor_scalar(src_hi, src_i, 4, None, ALU.logical_shift_right))
            step(dve.tensor_copy(bin_f, src_hi))
            step(dve.tensor_tensor(onehot_bin, bin_f.unsqueeze(1).to_broadcast([P, NBIN, EC]),
                                   iota_bin[:, :].unsqueeze(2).to_broadcast([P, NBIN, EC]), ALU.is_equal))
            flat_oh = onehot_bin.rearrange("p b e -> p (b e)")
            flat_run = running.rearrange("p b e -> p (b e)")
            step(dve.tensor_tensor_scan(flat_run, flat_oh, flat_oh, 0.0, ALU.add, ALU.max))
            step(dve.memset(bin_cum[:, 0:1], 0.0))
            step(dve.memset(bin_base[:, 0:1], 0.0))
            step(dve.tensor_copy(bin_cum[:, 1:NBIN + 1], running[:, :, EC - 1:EC].rearrange("p b e -> p (b e)")))
            dve.tensor_tensor(bin_cnt[:, :], bin_cum[:, 1:NBIN + 1], bin_cum[:, 0:NBIN], ALU.subtract).then_inc(cnt_ready, 1)
            dve.wait_ge(attr_in, 16)
            dve.tensor_reduce(bias_max[:, :], attr_sb.rearrange("p e h -> p h e"), AX, ALU.max).then_inc(pmax_ready, 1)

            dve.wait_ge(cnt_mm, 1)
            step(dve.tensor_scalar(bin_slots_i[:, :], ps[:, 7, NBIN:2 * NBIN], float(P - 1), None, ALU.add))
            step(dve.tensor_scalar(bin_slots_s[:, :], bin_slots_i[:, :], 7, None, ALU.logical_shift_right))
            step(dve.tensor_copy(bin_slots[:, :], bin_slots_s[:, :]))
            step(dve.tensor_tensor_scan(bin_base[:, 1:NBIN + 1], bin_slots[:, :], bin_slots[:, :], 0.0, ALU.add, ALU.max))
            step(dve.scalar_tensor_tensor(bin_off[:, :], bin_base[:, 0:NBIN], float(P), ps[:, 7, 0:NBIN], ALU.mult, ALU.add))
            dve.sem_inc(bins_read, 1)
            step(dve.scalar_tensor_tensor(bin_off[:, :], bin_off[:, :], -1.0, bin_cum[:, 0:NBIN], ALU.add, ALU.subtract))
            step(dve.tensor_tensor(running, running, bin_off[:, :].unsqueeze(2).to_broadcast([P, NBIN, EC]), ALU.add))
            step(dve.tensor_tensor(running, running, onehot_bin, ALU.mult))
            step(dve.tensor_reduce(pos, running.rearrange("p b e -> p e b"), AX, ALU.add))
            step(dve.tensor_copy(pos_i, pos))
            step(dve.tensor_scalar(pos_lo, pos_i, P - 1, None, ALU.bitwise_and))
            step(dve.tensor_scalar(pos_hi, pos_i, 7, None, ALU.logical_shift_right))
            step(dve.scalar_tensor_tensor(edge_idx, pos_lo, float(NS), pos_hi, ALU.mult, ALU.add))
            step(dve.tensor_scalar(src_lo, src_i, BIN - 1, None, ALU.bitwise_and))
            for f, v in ((0, dst_i), (1, src_lo), (2, typ_i)):
                step(dve.tensor_copy(fields[:, :, f:f + 1].rearrange("p e f -> p (e f)"), v))
            step(dve.memset(fields[:, :, 3:4], 0.0))
            dve.wait_ge(top_ready, 1)
            dve.tensor_tensor(fields[:, :, 4:FIELDS], attr_sb, bias_top[:, :].unsqueeze(1).to_broadcast([P, EC, H]),
                              ALU.subtract).then_inc(idx_ready, 1)

            def norm(n, v, to, ready, arrive):
                def finish(c):
                    dve.wait_ge(std_ready, NC * n + c + 1)
                    step(dve.reciprocal(rstd[:, c:c + 1], rstd[:, c:c + 1]))
                    dve.tensor_scalar(to[:, c, :], v[:, c, :], mv[:, c, 0:1], rstd[:, c:c + 1], ALU.subtract, ALU.mult)\
                       .then_inc(ready, 1)

                for c in range(NC):
                    arrive(c)
                    step(dve.bn_stats(stats[:, c, :], v[:, c, :]))
                    step(dve.bn_aggr(mv[:, c, :], stats[:, c, :]))
                    dve.tensor_scalar(rstd[:, c:c + 1], mv[:, c, 1:2], EPS, None, ALU.add).then_inc(var_ready, 1)
                    if c >= 1:
                        finish(c - 1)
                finish(NC - 1)

            dve.wait_ge(x_in, 16)
            norm(0, x0, z, z_ready, lambda c: None)

            dve.wait_ge(consts, n_consts)
            step(dve.tensor_scalar(group_diff[:, :, :], group_diff[:, :, :], GROUPS - 1, None, ALU.bitwise_and))
            step(dve.tensor_scalar(group_mask[:, :, :], group_diff[:, :, :], 0.0, None, ALU.is_equal))
            dve.wait_ge(small_in, 48)
            for layer in range(2):
                dve.tensor_tensor(
                    zero_blk[0:BP, layer, 0:TYPES * GROUPS].rearrange("p (t g) -> p t g", t=TYPES), group_mask[0:BP, :, :],
                    att_sb[:, layer, :].unsqueeze(2).to_broadcast([BP, TYPES, GROUPS]), ALU.mult).then_inc(att_ready, 1)
            step(dve.tensor_copy(ident_b[:, :], ident[:, :]))
            dve.tensor_scalar(bq_scaled[:, :], colv[:, 8:12], -SCALE, None, ALU.mult).then_inc(bq_ready, 1)

            cmp = dense[0:1, 0:NS * NBIN].rearrange("p (s b) -> p s b", b=NBIN)
            step(dve.tensor_tensor(cmp, bin_base[0:1, 0:NBIN].unsqueeze(1).to_broadcast([1, NS, NBIN]),
                                   iota_slot[:, :].unsqueeze(2).to_broadcast([1, NS, NBIN]), ALU.is_le))
            slot_f = dense[0:1, NS * NBIN:NS * NBIN + NS]
            step(dve.tensor_reduce(slot_f, cmp, AX, ALU.add))
            step(dve.tensor_scalar(slot_off[:, :], slot_f, -1.0, float(BIN), ALU.add, ALU.mult))

            for c in range(NC):
                dve.wait_ge(v_mm, c + 1)
                dve.tensor_tensor(v1[:, c, :, 0:3:2, :], ps[:, 4 + c, :].rearrange("p (m e d) -> p m e d", e=2, d=D),
                                  bv_row.rearrange("p (m e d) -> p m e d", e=2, d=D), ALU.add).then_inc(v_ev, 1)

            dve.wait_ge(v_ev, NC)
            step(dve.memset(dense[:, :], 0.0))

            dve.wait_ge(sorted_in, 16)
            step(dve.memset(edges[:, NS:NS + 2, :], 0.0))
            hi, mid, lo = (factors[:, :, a:a + H] for a in (0, H + TYPES, 2 * H + TYPES))
            step(dve.tensor_tensor(in_bin, edges[:, 0:NS, 1:2].to_broadcast([P, NS, BIN]),
                                   iota_src[:, :].unsqueeze(1).to_broadcast([P, NS, BIN]), ALU.is_equal))
            step(dve.tensor_scalar(factors[:, :, H:H + 1], edges[:, 0:NS, 2:3], 0.0, None, ALU.is_equal))
            step(dve.tensor_scalar(factors[:, :, H + 1:H + 2], edges[:, 0:NS, 2:3], 0.0, None, ALU.not_equal))
            dve.wait_ge(w_exp, 1)
            step(dve.tensor_copy(hi, weight_f))
            step(dve.tensor_tensor(weight_f, weight_f, hi, ALU.subtract))
            step(dve.tensor_copy(mid, weight_f))
            step(dve.tensor_tensor(weight_f, weight_f, mid, ALU.subtract))
            dve.tensor_copy(lo, weight_f).then_inc(factor_ready, 1)
            dve.wait_ge(factor_ready, 1)

            def target(s, k):
                dve.tensor_scalar(targets[:, k, :], iota_node[:, :], edges[:, bass.ds(s, 1), 0:1].rearrange("p s f -> p (s f)"),
                                  None, ALU.is_equal).then_inc(target_ready, 1)

            dve.sem_inc(slot_added, ADDED0)
            target(0, 0)
            target(1, 1)
            with dve.Fori(*span(0, NS, 8)) as s:
                for k in range(8):
                    target(s + (k + 2), (k + 2) % 4)
                    offset = dve.value_load(slot_off[0:1, bass.ds(s + k, 1)], min_val=0, max_val=N - BIN)
                    dve.wait_ge(slot_mm, s + (k + 1 + MM0))
                    dve.wait_ge(slot_added, s + (k + ADDED0))
                    to = mats.rearrange("p c a r -> p (c a) r")[:, :, bass.ds(offset, BIN)]\
                        .rearrange("p (b a) r -> p b a r", b=2)
                    got = ps[:, 2 * (k % 2):2 * (k % 2) + 2, 0:2 * HI_W].rearrange("p b (a r) -> p b a r", r=BIN)
                    dve.tensor_tensor(to, got, to, ALU.add).then_inc(slot_added, 1)
            dve.wait_ge(slot_added, NS + ADDED0)

            for c in range(NC):
                step(dve.tensor_tensor(none_t[:, c, :], mats[:, c, H, :], mats[:, c, H + 1, :], ALU.add))
                dve.tensor_scalar(none_t[:, c, :], none_t[:, c, :], 0.0, NO_EDGE, ALU.is_equal, ALU.mult).then_inc(none_ready, 1)

            def largest(k):
                h, r = divmod(k, NC)
                dve.wait_ge(score_mm, k + 1)
                dve.tensor_tensor_reduce(out=ps[:, r, :], in0=ps[:, r, :], in1=none[:, r, :], scale=1.0, scalar=NO_EDGE,
                                         op0=ALU.add, op1=ALU.min, accum_out=neg_max[:, h, r:r + 1]).then_inc(max_ready, 1)

            def prob(k):
                h, c = divmod(k, NC)
                dve.wait_ge(exp_mm, k + 1)
                if h >= 1:
                    dve.wait_ge(value_mm, k + 1 - NC)
                dve.tensor_tensor(probs[:, c, :], ps[:, 4 + k % 2, :], mats[:, c, h, :], ALU.mult).then_inc(prob_done, 1)

            def head_out(h):
                o, e = ps[:, 6 + h % 2, :], h % 2
                mine, others = slice(D * e, D * e + D), slice(D * (1 - e), D * (1 - e) + D)
                dve.wait_ge(value_mm, NC * (h + 1))
                step(dve.tensor_scalar(inv_sum[mine], o[others], TINY, None, ALU.max))
                step(dve.reciprocal(inv_sum[mine], inv_sum[mine]))
                dve.tensor_tensor(heads_t[mine, h // 2, :], o[mine], inv_sum[mine], ALU.mult).then_inc(head_done, 1)
                dve.wait_ge(head_done, h + 1)

            dve.wait_ge(none_ev, NC)
            for k in range(STEPS + VALUE_LAG + 1):
                if k < STEPS:
                    largest(k)
                if 0 <= k - EXP_LAG < STEPS:
                    prob(k - EXP_LAG)
                if k - VALUE_LAG > 0 and (k - VALUE_LAG) % NC == 0:
                    head_out((k - VALUE_LAG) // NC - 1)
                if k == STEPS:
                    dve.wait_ge(late_in, 16)
                if STEPS <= k < STEPS + NC:
                    step(dve.tensor_tensor(x0[:, k - STEPS, :], x0[:, k - STEPS, :], row4[:, 0, :], ALU.add))

            def bring_x1(c):
                dve.wait_ge(x1_mm, c + 1)
                step(dve.tensor_tensor(x1[:, c, :], ps[:, 4 + c, :], x0[:, c, :], ALU.add))

            norm(1, x1, z2, z2_ready, bring_x1)
            for c in range(NC):
                step(dve.tensor_tensor(x0[:, c, :], x0[:, c, :], row4[:, 0, :], ALU.subtract))
                step(dve.tensor_tensor(x0[:, c, :], x0[:, c, :], x1[:, c, :], ALU.add))
                step(dve.tensor_tensor(x0[:, c, :], x0[:, c, :], row4[:, 1, :], ALU.add))

            def bring_x2(c):
                dve.wait_ge(x2_mm, c + 1)
                step(dve.tensor_tensor(x0[:, c, :], ps[:, c, :], x0[:, c, :], ALU.add))

            norm(2, x0, y, y_ready, bring_x2)

            def gate_dots(layer, v, c):
                for t in range(TYPES):
                    ins = dve.tensor_tensor_reduce(out=junk[:, t, :], in0=v[:, c, :], in1=gate_rows[:, TYPES * layer + t, :],
                                                   scale=1.0, scalar=0.0, op0=ALU.mult, op1=ALU.add,
                                                   accum_out=gate_dot[:, c, t:t + 1])
                    if (c, t) == (NC - 1, TYPES - 1):
                        ins.then_inc(gate_ready, 1)
                    else:
                        step(ins)

            dve.wait_ge(gates_in, 16)
            dve.wait_ge(y_ready, NC)
            for c in range(NC):
                gate_dots(0, y, c)
            for c in range(NC):
                dve.wait_ge(agg_mm, c + 1)
                step(dve.tensor_tensor(g1_out[:, c, :], ps[:, c, :], row4[:, 2, :], ALU.add))
                dve.tensor_scalar(g1_out[:, c, :], g1_out[:, c, :], 0.0, None, ALU.max).then_inc(g1_ready, 1)
                dve.wait_ge(g1_ready, c + 1)
                if c == 0:
                    dve.wait_ge(gate_ev, 1)
                gate_dots(1, g1_out, c)
            for c in range(NC):
                step(dve.tensor_tensor(y[:, c, :], y[:, c, :], row4[:, 3, :], ALU.add))

            def bring_out(c):
                dve.wait_ge(agg_mm, NC + c + 1)
                step(dve.tensor_tensor(x0[:, c, :], ps[:, c, :], y[:, c, :], ALU.add))

            norm(3, x0, g1_out, out_ready, bring_out)

        @block.tensor
        def _(pe):
            mm = nc.tensor.matmul

            def transpose_rows(v, r, bank, ready, done):
                pe.wait_ge(ready, r + 1)
                for c in range(NC):
                    last = nc.tensor.transpose(ps[:, bank + c, r * P:(r + 1) * P], v[:, r, c * P:(c + 1) * P], ident[:, :])
                last.then_inc(done, 1)

            def product(bank, pairs, done=None, start=True, stop=True):
                for i, (l, r) in enumerate(pairs):
                    last = mm(ps[:, bank, :], l, r, start=start and i == 0, stop=stop and i == len(pairs) - 1)
                if done is not None:
                    last.then_inc(done, 1)

            def then_transposes(make, v, bank, ready, done):
                for n in range(NC):
                    make(n)
                    if n >= 1:
                        transpose_rows(v, n - 1, bank, ready, done)
                transpose_rows(v, NC - 1, bank, ready, done)

            def basis_tile(layer, k, n, turn):
                pe.wait_ge(basis_in[k], turn)
                pe.wait_ge(basis_ev, n + 1)
                for j in range(TILE_ROWS):
                    last = mm(ps[32 * j:32 * j + 32, 4 + k % 2, :], zero_blk[0:BP, layer, :],
                              ring[0:BP, k, j * C:(j + 1) * C], start=True, stop=True)
                last.then_inc(basis_mm, 1)

            pe.sem_inc(basis_mm, TILE0)
            pe.sem_inc(slot_mm, MM0)
            pe.wait_ge(consts, n_consts)
            pe.wait_ge(cnt_ready, 1)
            mm(ps[:, 7, 0:NBIN], tri[:, :], bin_cnt[:, :], start=True, stop=True)
            mm(ps[:, 7, NBIN:2 * NBIN], ones[:, :], bin_cnt[:, :], start=True, stop=True).then_inc(cnt_mm, 1)
            for r in range(NC):
                transpose_rows(z, r, 0, z_ready, z_mm)
            pe.wait_ge(wqkv_in, 48)
            pe.wait_ge(z_ev, NC)
            pe.wait_ge(bins_read, 1)
            for g in range(2 * NC):
                kind, m = divmod(g, NC)
                product((4, 0)[kind] + m, [(wqkv[:, kind, c, m * P:(m + 1) * P], z_t[:, c, :]) for c in range(NC)], qk_mm)
            for n in range(NC):
                pe.wait_ge(qk_ev, 2 * (n + 1))
                product(4 + n, [(z_t[:, c, n * P:(n + 1) * P], wqkv[:, 2, c, :]) for c in range(NC)], v_mm)
            pe.wait_ge(v_ev, 2)
            pe.wait_ge(att_ready, 2)
            with pe.Fori(*span(0, TILES, RING)) as m:
                for k in range(RING):
                    basis_tile(0, k, m + k, m * (16 // RING) + 16)

            def slot(s, k):
                pe.wait_ge(target_ready, s + (k + 1))
                pe.wait_ge(rhs_ready, s + (k + 1))
                pe.wait_ge(slot_added, s + (k + 1))
                for c in range(NC):
                    o = ps[:, 2 * (k % 2) + c // 2, HI_W * (c % 2):HI_W * (c % 2) + HI_W]
                    t = targets[:, k % 4, c * P:(c + 1) * P]
                    mm(o, t, rhs[:, k % 4, 0:HI_W], start=True, stop=False)
                    mm(o[:, 0:LO_W], t, rhs[:, k % 4, HI_W:HI_W + LO_W], start=False, stop=False)
                    last = mm(o[:, 0:LO_W], t, rhs[:, k % 4, HI_W + LO_W:RHS_W], start=False, stop=True)
                last.then_inc(slot_mm, 1)

            with pe.Fori(*span(0, TILED, SLOT_TURN)) as s:
                for k in range(SLOT_TURN):
                    slot(s, k)
                    if k % 4 == 3:
                        t = k // 4
                        m = s // (SLOT_TURN // RING) + t
                        basis_tile(1, t, m + TILES, s + (TILES * 16 // RING + 16))
            with pe.Fori(*span(TILED, NS, 4)) as s:
                for k in range(4):
                    slot(s, k)

            pe.wait_ge(slot_added, NS + ADDED0)
            for r in range(NC):
                transpose_rows(none_t, r, 0, none_ready, none_mm)
            pe.wait_ge(basis_ev, 2 * TILES + EV0)

            def scores(k):
                h, r = divmod(k, NC)
                if h == 0:
                    pe.wait_ge(none_ev, r + 1)
                else:
                    pe.wait_ge(exp_done, k + 1 - NC)
                mm(ps[:, r, :], q_t[:, h, r * P:(r + 1) * P], k_t[:, h // 2, :], start=True, stop=True).then_inc(score_mm, 1)

            def transpose_exps(k):
                h, c = divmod(k, NC)
                pe.wait_ge(exp_done, NC * (h + 1))
                if k >= 2:
                    pe.wait_ge(prob_done, k - 1)
                for r in range(NC):
                    last = nc.tensor.transpose(ps[:, 4 + k % 2, r * P:(r + 1) * P], exps[:, h % 2, r, c * P:(c + 1) * P],
                                               ident[:, :])
                last.then_inc(exp_mm, 1)

            def values(k):
                h, c = divmod(k, NC)
                pe.wait_ge(prob_done, k + 1)
                if h >= 2 and c == 0:
                    pe.wait_ge(head_done, h - 1)
                mm(ps[:, 6 + h % 2, :], v1[:, c, h // 2, h % 2:h % 2 + 2, :].rearrange("p a d -> p (a d)"), probs[:, c, :],
                   start=c == 0, stop=c == NC - 1).then_inc(value_mm, 1)

            for k in range(STEPS + VALUE_LAG):
                if k < STEPS:
                    scores(k)
                if 0 <= k - EXP_LAG < STEPS:
                    transpose_exps(k - EXP_LAG)
                if k >= VALUE_LAG:
                    values(k - VALUE_LAG)

            pe.wait_ge(wo_in, 16)
            pe.wait_ge(head_done, H)
            then_transposes(lambda n: product(4 + n, [(heads_t[:, c, n * P:(n + 1) * P], wo_sb[:, c, :])
                                                      for c in range(NC)], x1_mm),
                            z2, 0, z2_ready, z2_mm)
            pe.wait_ge(w1_in, 16)
            for m in range(NH):
                if m == 0:
                    pe.wait_ge(z2_ev, NC)
                if m >= 4:
                    pe.wait_ge(h1_ev, m - 3)
                product(4 + m % 4, [(w1_sb[:, c, m * P:(m + 1) * P], z2_t[:, c, :]) for c in range(NC)], h1_mm)
            pe.wait_ge(w2_in, 16 * NC)
            pe.wait_ge(h1_ev, NH)
            then_transposes(lambda n: product(n, [(h1_t[:, m, n * P:(n + 1) * P], w2_sb[:, m // 2, m % 2, :])
                                                  for m in range(NH)], x2_mm),
                            y, 4, y_ready, y_mm)
            for layer in range(2):
                in_t = (y_t, g1_t)[layer]
                root, w = ((root_a, w_a), (root_b, w_b))[layer]
                pe.wait_ge((y_ev, g1_ev)[layer], NC)
                pe.wait_ge((wa_in, wb_in)[layer], 16 * (NC + 1))
                for n in range(NC):
                    product(n, [(in_t[:, c, n * P:(n + 1) * P], root[:, c, :]) for c in range(NC)], stop=False)
                for g in range(TYPES * NC):
                    t, n = divmod(g, NC)
                    if g >= 4:
                        pe.wait_ge(msg_ev, TYPES * NC * layer + g - 3)
                    product(4 + n, [(in_t[:, c, n * P:(n + 1) * P], w[:, c, t, :]) for c in range(NC)], msg_mm)
                pe.wait_ge(msg_ev, TYPES * NC * (layer + 1))

                def aggregate(n):
                    product(n, [(mats[:, c, H + t, n * P:(n + 1) * P], msgs[:, t, c, :]) for t in range(TYPES)
                                for c in range(NC)], agg_mm, start=False)

                if layer == 0:
                    then_transposes(aggregate, g1_out, 4, g1_ready, g1_mm)
                else:
                    for n in range(NC):
                        aggregate(n)


def kernel(**inputs):
    import numpy as np
    import concourse.bacc as bacc
    from concourse.bass_utils import run_bass_kernel_spmd

    def a(name):
        return np.ascontiguousarray(np.asarray(inputs[name]))

    def column(v):
        return v.reshape(-1, P).T

    gates = np.concatenate([a(f"L1_gnn_gate_w{i}").reshape(TYPES, C) for i in (1, 2)])
    att = np.stack([np.repeat(a(f"L1_gnn_att{i}").T, GROUPS, axis=0) for i in (1, 2)], axis=1)
    arrays = {
        "x": a("x"), "src": a("src").reshape(P, EC), "dst": a("dst").reshape(P, EC),
        "etype": a("edge_type_2").reshape(P, EC), "attr": a("edge_attr_8").reshape(P, EC, H),
        "cols": np.concatenate([column(a(n)) for n in COLS], axis=1),
        "rows": np.stack([a(n) for n in ROWS]),
        "wq": a("L0_gnn_Wq"), "wk": a("L0_gnn_Wk"), "wv": a("L0_gnn_Wv"), "wo": a("L0_gnn_Wo"),
        "w1": a("L0_gnn_W1"), "w2": a("L0_gnn_W2"),
        "basis1": a("L1_gnn_basis1"), "basis2": a("L1_gnn_basis2"), "att": att,
        "gates": gates, "root1": a("L1_gnn_root1"), "root2": a("L1_gnn_root2"),
    }
    arrays = {k: np.ascontiguousarray(v) for k, v in arrays.items()}
    nc = bacc.Bacc("TRN2", target_bir_lowering=False, num_devices=1)
    t = {k: nc.dram_tensor(k, v.shape, mybir.dt.from_np(v.dtype), kind="ExternalInput").ap() for k, v in arrays.items()}
    out = nc.dram_tensor("out", (N, C), F32, kind="ExternalOutput").ap()
    build(nc, t["x"], t["src"], t["dst"], t["etype"], t["attr"], t["cols"], t["rows"], t["wq"], t["wk"], t["wv"],
          t["wo"], t["w1"], t["w2"], [t["basis1"], t["basis2"]], t["att"], t["gates"], [t["root1"], t["root2"]], out)
    r = run_bass_kernel_spmd(nc, [arrays], core_ids=[0])
    return r.results[0]["out"]
```

```python
from contextlib import ExitStack

import concourse.bass as bass
from concourse import mybir

F32, BF16, F16 = mybir.dt.float32, mybir.dt.bfloat16, mybir.dt.float16
I32, U32 = mybir.dt.int32, mybir.dt.uint32
ALU = mybir.AluOpType
ACT = mybir.ActivationFunctionType
AX = mybir.AxisListType.X
RMAX = bass.bass_isa.ReduceOp.max

P = 128
N = 512
C = 512
NC = C // P
H = 8
D = C // H
HID = 1024
NH = HID // P
HALF = N // 2
EDGES = 16384
EC = EDGES // P
TYPES = 2
BASES = 30
EPS = 1e-5
QKV_BANKS = (0, 1, 2, 3, 6, 7)
SCALE = 1.0 / 8.0

BIN = 16
NBIN = N // BIN
GROUP = 2 * P
NS = 192
PAIRS = NS // 2
DVE_SLOTS = 32
FIELDS = 15
AHEAD, DVE_TURN = 4, 2
FIRST_SLOTS = 16
FIRST = 24
SLOT_TURN, TILED = 16, 64
NM = H + TYPES
UW = 3 * H + TYPES
HI_W, LO_W = NM * BIN, H * BIN
RHS_W = UW * BIN

GROUPS = 4
BP = GROUPS * BASES
TILE_ROWS = 4
TILES = C // GROUPS // TILE_ROWS
POOL_WORDS = 8192
SLOT_RING = 8
RING = 4
NO_EDGE = 2.0 ** 100
TINY = 1e-37
STEPS = H * NC
EXP_LAG, VALUE_LAG = 5, 7
INVERT_LAG = VALUE_LAG + 2 * NC + 1
ADDED0, MM0, TILE0, EV0 = 4, SLOT_RING, RING, 2

COLS = ["L0_gnn_ln1_g", "L0_gnn_ln1_b", "L0_gnn_bq", "L0_gnn_bk", "L0_gnn_ln2_g", "L0_gnn_ln2_b", "L0_gnn_b1"]
ROWS = ["L0_gnn_bv", "L0_gnn_bo", "L0_gnn_b2", "L1_gnn_bias1", "L1_gnn_bias2"]


def span(start, end, step):
    return start, end - step + 1, step


def build(nc, x, src, dst, etype, attr, cols, rows, wq, wk, wv, wo, w1, w2, basis, att, gates, roots, out):
    edge_rows = nc.dram_tensor("edge_rows", (NS * P, FIELDS), F32).ap()
    w_rows = nc.dram_tensor("w_rows", (2, TYPES * GROUPS, P, C), F32).ap()

    ctx = ExitStack()
    with ctx:
        def sb(name, shape, dt=F32):
            return ctx.enter_context(nc.sbuf_tensor(name, shape, dt))

        def sem(name):
            return ctx.enter_context(nc.semaphore(name))

        dense = sb("dense", [P, NC * NM * N])
        mats = dense[:, :].rearrange("p (c a r) -> p c a r", c=NC, a=NM)
        qk = sb("qk", [P, 2 * H * N])
        q_t = qk[:, 0:H * N].rearrange("p (h n) -> p h n", h=H)
        k_t, heads_t = (qk[:, a * N:(a + NC) * N].rearrange("p (c n) -> p c n", c=NC) for a in (H, H + NC))
        tri, ones = heads_t[:, 0, 0:P], heads_t[:, 0, P:2 * P]
        v1 = sb("v1", [P, NC, H // 2, 3, D])
        x0 = sb("x0", [P, NC, C])
        ring = sb("ring", [P, RING, TILE_ROWS * C])
        wrows = sb("wrows", [P, 2, 2, C])
        pool_mem = sb("pool_mem", [P, POOL_WORDS])
        stage_idx = sb("stage_idx", [P, 2, 8], U32)
        stage_row = sb("stage_row", [P, 2, 8, FIELDS])
        ident = sb("ident", [P, P])
        att_blk = sb("att_blk", [P, 2, 32])
        iota_node = sb("iota_node", [P, N], F16)
        iota_bin = sb("iota_bin", [P, NBIN], F16)
        iota_src = sb("iota_src", [P, BIN], BF16)
        group_diff = sb("group_diff", [P, TYPES, GROUPS], I32)
        group_mask = sb("group_mask", [P, TYPES, GROUPS])
        att_sb = sb("att_sb", [BP, 2, TYPES])
        colv = sb("colv", [P, 4 * 6 + 8])
        bq_scaled = sb("bq_scaled", [P, NC])
        stats = sb("stats", [P, NC, 6])
        mv = sb("mv", [P, NC, 2])
        rstd = sb("rstd", [P, NC])
        neg_max = sb("neg_max", [P, H, NC])
        gate_dot = sb("gate_dot", [P, NC, TYPES])
        gate = sb("gate", [P, NC, TYPES])
        pair_off = sb("pair_off", [1, PAIRS], I32)
        ps = ctx.enter_context(nc.psum_tensor("ps", [P, 8, 512], F32))

        def carve(base, start, shape, dt=F32):
            n = 1
            for s in shape:
                n *= s
            size = n * (2 if dt in (BF16, F16) else 4) // 4
            v = base[:, start:start + size]
            v = v if dt == F32 else v.bitcast(dt)
            if len(shape) == 2:
                v = v.rearrange("p (a b) -> p a b", a=shape[0])
            elif len(shape) == 3:
                v = v.rearrange("p (a b c) -> p a b c", a=shape[0], b=shape[1])
            return v, start + size

        onehot_bin, at = carve(dense, 0, [NBIN, EC], F16)
        running, at = carve(dense, at, [NBIN, EC], F16)
        places, at = carve(dense, at, [NBIN, EC])
        wqkv, at = carve(dense, at, [3, NC, C])
        z, at = carve(dense, at, [NC, C])
        z_t, at = carve(dense, at, [NC, N])
        bv_row, at = carve(dense, at, [C])
        weight_f, at = carve(dense, at, [EC, H])
        bin_cum, at = carve(dense, at, [NBIN + 1])
        bin_base, at = carve(dense, at, [NBIN + 1])
        bin_cnt, at = carve(dense, at, [NBIN])
        bin_pairs_i, at = carve(dense, at, [NBIN], I32)
        bin_pairs_s, at = carve(dense, at, [NBIN], I32)
        bin_pairs, at = carve(dense, at, [NBIN])
        bin_off, at = carve(dense, at, [NBIN])
        bias_max, at = carve(dense, at, [H])
        bias_top, at = carve(dense, at, [H])
        iota_pair, at = dense[0:1, at:at + PAIRS], at + PAIRS
        assert at <= NC * NM * N
        src_i, at = carve(pool_mem, 0, [EC], I32)
        dst_i, at = carve(pool_mem, at, [EC], I32)
        typ_i, at = carve(pool_mem, at, [EC], I32)
        attr_sb, at = carve(pool_mem, at, [EC, H])
        fields, at = carve(pool_mem, at, [EC, FIELDS])
        src_lo, at = carve(pool_mem, at, [EC], I32)
        src_hi, at = carve(pool_mem, at, [EC], I32)
        bin_f, at = carve(pool_mem, at, [EC], F16)
        pos, at = carve(pool_mem, at, [EC])
        pos_i, at = carve(pool_mem, at, [EC], I32)
        pos_lo, at = carve(pool_mem, at, [EC], I32)
        pos_hi, at = carve(pool_mem, at, [EC], I32)
        edge_idx, at = carve(pool_mem, at, [EC], U32)
        filler, at = carve(pool_mem, at, [NS // 2, FIELDS])
        fields_b = fields.rearrange("p e f -> p (e f)").bitcast(BF16).rearrange("p (e f) -> p e f", e=EC)
        assert at <= POOL_WORDS
        edges, at = carve(pool_mem, 0, [NS + AHEAD, FIELDS])
        edges_b = edges.rearrange("p s f -> p (s f)").bitcast(BF16).rearrange("p (s f) -> p s f", s=NS + AHEAD)
        targets, at = carve(pool_mem, at, [SLOT_RING, N], BF16)
        rhs, at = carve(pool_mem, at, [SLOT_RING, RHS_W], BF16)
        in_bin, at = carve(pool_mem, at, [NS, BIN], BF16)
        assert at <= POOL_WORDS
        exps, at = carve(pool_mem, 0, [2, NC, N])
        probs, at = carve(pool_mem, at, [NC, N])
        inv_sum, at = carve(pool_mem, at, [N])
        none_t, none = probs, ring[:, 3, :].rearrange("p (c n) -> p c n", c=NC)
        row4 = wrows[:, :, :, :].rearrange("p a b n -> p (a b) n")
        wo_sb = ring[:, 0, :].rearrange("p (c n) -> p c n", c=NC)
        w1_sb = ring[:, 1:3, :].rearrange("p a n -> p (a n)").rearrange("p (c n) -> p c n", c=NC)
        w2_sb, root_a, w_a = mats[:, :, 0:2], mats[:, :, 2], mats[:, :, 3:5]
        w_b, root_b = mats[:, :, 5:7], mats[:, :, 7]
        z2, z2_t, x1 = q_t[:, 0:4], q_t[:, 4:8], k_t
        h1_t = exps[:, :, :, :].rearrange("p a c n -> p (a c) n")
        msgs, (junk, at) = exps, carve(pool_mem, H * N, [2, N])
        gate_rows, at = carve(pool_mem, at, [2 * TYPES, C])
        y, y_t, g1_out, g1_t = z2, z2_t, x1, heads_t
        assert at <= POOL_WORDS

        src_in, edges_in, attr_in, x_in, small_in = sem("src_in"), sem("edges_in"), sem("attr_in"), sem("x_in"), sem("small_in")
        wqkv_in = sem("wqkv_in")
        consts, bin_const = sem("consts"), sem("bin_const")
        filled, fill_done, pool_done = sem("filled"), sem("fill_done"), sem("pool_done")
        dve_done = sem("dve_done")
        att_ready = sem("att_ready")
        basis_in = [sem(f"basis_in{i}") for i in range(RING)]
        basis_mm, basis_ev = sem("basis_mm"), sem("basis_ev")
        w_out = [sem(f"w_out{i}") for i in range(2)]
        pmax_ready, top_ready, weight_ready = sem("pmax_ready"), sem("top_ready"), sem("weight_ready")
        bins_read, bq_ready = sem("bins_read"), sem("bq_ready")
        cnt_ready, cnt_mm, idx_ready, fields_ready = sem("cnt_ready"), sem("cnt_mm"), sem("idx_ready"), sem("fields_ready")
        src_lo_ready, dve_fields = sem("src_lo_ready"), sem("dve_fields")
        staged, stage_go = sem("staged"), sem("stage_go")
        scattered = [sem(f"scattered{i}") for i in range(2)]
        first_in, sorted_in = sem("first_in"), sem("sorted_in")
        table_in = sem("table_in")
        var_ready, std_ready = sem("var_ready"), sem("std_ready")
        z_ready, z_mm, z_ev = sem("z_ready"), sem("z_mm"), sem("z_ev")
        qk_mm, qk_ev, v_mm, v_ev = sem("qk_mm"), sem("qk_ev"), sem("v_mm"), sem("v_ev")
        in_bin_ready = sem("in_bin_ready")
        target_ready = sem("target_ready")
        rhs_ready, last_rhs_ready, slot_mm, slot_added = sem("rhs_ready"), sem("last_rhs_ready"), sem("slot_mm"), sem("slot_added")
        none_ready, none_mm, none_ev = sem("none_ready"), sem("none_mm"), sem("none_ev")
        score_mm, max_ready, exp_done = sem("score_mm"), sem("max_ready"), sem("exp_done")
        exp_mm, prob_done, value_mm = sem("exp_mm"), sem("prob_done"), sem("value_mm")
        head_sums, sums_kept, inverted, head_done = sem("head_sums"), sem("sums_kept"), sem("inverted"), sem("head_done")
        late_in, wo_in, w1_in, w2_in = sem("late_in"), sem("wo_in"), sem("w1_in"), sem("w2_in")
        wa_in, wb_in = sem("wa_in"), sem("wb_in")
        x1_mm, gates_in = sem("x1_mm"), sem("gates_in")
        z2_ready, z2_mm, z2_ev = sem("z2_ready"), sem("z2_mm"), sem("z2_ev")
        h1_mm, h1_ev, x2_mm = sem("h1_mm"), sem("h1_ev"), sem("x2_mm")
        y_ready, y_mm, y_ev = sem("y_ready"), sem("y_mm"), sem("y_ev")
        gate_ready, gate_ev = sem("gate_ready"), sem("gate_ev")
        msg_mm, msg_ev, agg_mm = sem("msg_mm"), sem("msg_ev"), sem("agg_mm")
        g1_ready, g1_mm, g1_ev = sem("g1_ready"), sem("g1_mm"), sem("g1_ev")
        out_ready, out_done = sem("out_ready"), sem("out_done")

        n_consts, early_consts = 11, 6

        def slot_rhs(eng, s, k):
            factors = edges_b[:, bass.ds(s + k, 1), 4:4 + UW].rearrange("p s a -> p (s a)")
            return eng.tensor_tensor(
                rhs[:, k % SLOT_RING, :].rearrange("p (a r) -> p a r", r=BIN), factors.unsqueeze(2).to_broadcast([P, UW, BIN]),
                in_bin[:, bass.ds(s + k, 1), :].to_broadcast([P, UW, BIN]), ALU.mult)

        def edge_fields(eng, e, done, base, last):
            hi, types, mid, lo = (fields_b[:, e, 4 + a:4 + b] for a, b in (
                (0, H), (H, H + TYPES), (H + TYPES, 2 * H + TYPES), (2 * H + TYPES, UW)))
            eng.tensor_copy(fields[:, e, 0:1].rearrange("p e f -> p (e f)"), dst_i[:, e]).then_inc(done, 1)
            eng.tensor_copy(fields[:, e, 1:2].rearrange("p e f -> p (e f)"), src_lo[:, e]).then_inc(done, 1)
            first, second = (types[:, :, t:t + 1].rearrange("p e f -> p (e f)") for t in range(TYPES))
            eng.tensor_scalar(first, typ_i[:, e], 0.0, None, ALU.is_equal).then_inc(done, 1)
            eng.tensor_tensor(mid, weight_f[:, e], hi, ALU.subtract).then_inc(done, 1)
            eng.wait_ge(done, base + 4)
            eng.tensor_scalar(second, first, -1.0, 1.0, ALU.mult, ALU.add).then_inc(done, 1)
            eng.tensor_tensor(weight_f[:, e], weight_f[:, e], hi, ALU.subtract).then_inc(done, 1)
            eng.wait_ge(done, base + 6)
            eng.tensor_tensor(lo, weight_f[:, e], mid, ALU.subtract).then_inc(last, 1)

        block = ctx.enter_context(nc.Block())

        @block.sync
        def _(sp):
            sp.dma_start(src_i, src).then_inc(src_in, 16)
            sp.dma_start(attr_sb, attr).then_inc(attr_in, 16)
            sp.dma_start(dst_i, dst).then_inc(edges_in, 16)
            sp.dma_start(typ_i, etype).then_inc(edges_in, 16)

            def load_tiles(layer, m):
                rows_of = basis[layer].rearrange("b (g i) o -> (b g) (i o)", g=GROUPS)
                for k in range(RING):
                    sp.wait_ge(basis_mm, m + (layer * TILES + k + 1))
                    sp.dma_start(ring[0:BP, k, :], rows_of[:, bass.ds((m + k) * (TILE_ROWS * C), TILE_ROWS * C)])\
                      .then_inc(basis_in[k], 16)

            def store_rows(layer, m):
                to = w_rows[layer].rearrange("g (m j) o -> g m j o", j=TILE_ROWS)
                for half in range(2):
                    sp.wait_ge(basis_ev, m + (layer * TILES + 2 * half + 2 + EV0))
                    for j in range(TILE_ROWS):
                        sp.dma_start(to[:, bass.ds(m + 2 * half, 2), j, :],
                                     wrows[32 * j:32 * j + TYPES * GROUPS, half, :, :]).then_inc(w_out[half], 16)

            load_tiles(0, 0)
            with sp.Fori(*span(RING, TILES, RING)) as m:
                load_tiles(0, m)
                store_rows(0, m - RING)
            load_tiles(1, 0)
            store_rows(0, TILES - RING)
            late = TILES - TILED // RING
            with sp.Fori(*span(RING, late, RING)) as m:
                load_tiles(1, m)
                store_rows(1, m - RING)
            sp.wait_ge(sorted_in, 16)
            with sp.Fori(*span(late, TILES, RING)) as m:
                load_tiles(1, m)
                store_rows(1, m - RING)
            store_rows(1, TILES - RING)

            sp.wait_ge(basis_mm, 2 * TILES + TILE0)
            sp.dma_start(wo_sb, wo.rearrange("(c p) n -> p c n", p=P)).then_inc(wo_in, 16)
            sp.dma_start(w1_sb, w1.rearrange("(c p) n -> p c n", p=P)).then_inc(w1_in, 16)
            for i in range(2):
                sp.wait_ge(w_out[i], 16 * 4 * (TILES // 2))
            sp.dma_start(row4, rows[1:5, :].unsqueeze(0).to_broadcast([P, 4, C])).then_inc(late_in, 16)
            sp.wait_ge(prob_done, 2 * NC)
            for c in range(NC):
                sp.dma_start(w2_sb[:, c], w2[2 * P * c:2 * P * (c + 1), :].rearrange("(k p) n -> p k n", p=P)).then_inc(w2_in, 16)
            for layer, (w_to, root_to, w_done) in enumerate(((w_a, root_a, wa_in), (w_b, root_b, wb_in))):
                sp.wait_ge(prob_done, (5, 8)[layer] * NC)
                for c in range(NC):
                    sp.dma_start(w_to[:, c], w_rows[layer].rearrange("(t c) p n -> p c t n", t=TYPES)[:, c]).then_inc(w_done, 16)
                sp.dma_start(root_to, roots[layer].rearrange("(c p) n -> p c n", p=P)).then_inc(w_done, 16)
            sp.wait_ge(head_done, H // 2)
            sp.dma_start(gate_rows, gates.unsqueeze(0).to_broadcast([P, 2 * TYPES, C])).then_inc(gates_in, 16)
            for c in range(NC):
                sp.wait_ge(out_ready, c + 1)
                sp.dma_start(out[c * P:(c + 1) * P, :], g1_out[:, c, :]).then_inc(out_done, 16)
            sp.wait_ge(out_done, 16 * NC)

        @block.gpsimd
        def _(pool):
            pool.iota(iota_bin[:, :], [[1, NBIN]], base=0, channel_multiplier=0,
                      allow_small_or_imprecise_dtypes=True).then_inc(bin_const, 1)
            pool.memset(ones[:, :], 1.0).then_inc(consts, 1)
            pool.memset(ident[:, :], 0.0).then_inc(consts, 1)
            pool.iota(group_diff[:, :, :], [[0, TYPES], [-1, GROUPS]], base=0, channel_multiplier=1).then_inc(consts, 1)
            pool.memset(att_blk[:, :, :], 0.0).then_inc(consts, 1)
            pool.wait_ge(consts, 4)
            pool.affine_select(out=tri[:, :], in_=ones[:, :], compare_op=ALU.is_gt, fill=0.0, base=0,
                               pattern=[[1, P]], channel_multiplier=-1).then_inc(consts, 1)
            pool.affine_select(out=ident[:, :], in_=ident[:, :], compare_op=ALU.not_equal, fill=1.0, base=0,
                               pattern=[[-1, P]], channel_multiplier=1).then_inc(consts, 1)
            pool.memset(filler, 0.0).then_inc(filled, 1)
            pool.wait_ge(filled, 1)
            pool.memset(filler[:, :, 1:2], -1.0).then_inc(filled, 1)
            pool.wait_ge(filled, 2)
            for half in range(2):
                pool.dma_start(edge_rows.rearrange("(k p s) f -> k p s f", k=2, p=P)[half], filler).then_inc(fill_done, 16)
            pool.iota(iota_node[:, :], [[1, N]], base=0, channel_multiplier=0,
                      allow_small_or_imprecise_dtypes=True).then_inc(consts, 1)
            pool.iota(iota_src[:, :], [[1, BIN]], base=0, channel_multiplier=0,
                      allow_small_or_imprecise_dtypes=True).then_inc(consts, 1)
            pool.iota(iota_pair[:, :], [[1, PAIRS]], base=0, channel_multiplier=0,
                      allow_small_or_imprecise_dtypes=True).then_inc(consts, 1)
            pool.memset(q_t, 0.0).then_inc(consts, 1)
            pool.memset(v1[:, :, :, 1, :], 1.0).then_inc(consts, 1)
            pool.wait_ge(pmax_ready, 1)
            pool.partition_all_reduce(bias_top, bias_max, P, RMAX).then_inc(pool_done, 1)
            pool.wait_ge(pool_done, 1)
            pool.tensor_scalar(bias_top, bias_top, -1.0, None, ALU.mult).then_inc(top_ready, 1)
            pool.wait_ge(edges_in, 32)
            pool.wait_ge(src_lo_ready, 1)
            pool.wait_ge(weight_ready, H + 1)
            edge_fields(pool, slice(0, FIRST), pool_done, 1, pool_done)

            pool.wait_ge(idx_ready, 1)
            pool.wait_ge(fill_done, 32)
            pool.wait_ge(pool_done, 1 + 7)

            def scatter(j, half, turn, n):
                if turn is not None:
                    pool.wait_ge(scattered[half], turn)
                pool.tensor_copy(stage_idx[:, half, :], edge_idx[:, bass.ds(j, 8)]).then_inc(staged, 1)
                pool.tensor_copy(stage_row[:, half, :, :], fields[:, bass.ds(j, 8), :]).then_inc(staged, 1)
                pool.wait_ge(staged, n)
                pool.sem_inc(stage_go, 1)
                for k in range(8):
                    pool.indirect_dma_start(
                        out=edge_rows, out_offset=bass.IndirectOffsetOnAxis(ap=stage_idx[:, half, k:k + 1], axis=0),
                        in_=stage_row[:, half, k, :], in_offset=None).then_inc(scattered[half], 16)

            for half in range(2):
                scatter(8 * half, half, None, 2 * half + 2)
            scatter(16, 0, 8 * 16, 6)
            pool.wait_ge(idx_ready, 2)
            pool.wait_ge(fields_ready, 1)
            scatter(24, 1, 8 * 16, 8)
            with pool.Fori(*span(32, EC, 16)) as j:
                for half in range(2):
                    scatter(j + 8 * half, half, j * 8, j // 4 + (2 * half + 2))

            for i in range(2):
                pool.wait_ge(scattered[i], EC // 2 * 16)
            by_slot = edge_rows.rearrange("(p s) f -> p s f", s=NS)
            pool.dma_start(edges[:, 0:FIRST_SLOTS, :], by_slot[:, 0:FIRST_SLOTS]).then_inc(first_in, 16)
            pool.dma_start(edges[:, FIRST_SLOTS:NS, :], by_slot[:, FIRST_SLOTS:NS]).then_inc(sorted_in, 16)

            def rhs_slots(start, end):
                with pool.Fori(*span(start, end, 8)) as s:
                    for k in range(7):
                        pool.wait_ge(slot_mm, s + (k + 1))
                        slot_rhs(pool, s, k).then_inc(rhs_ready, 2 if k == 6 else 1)

            pool.wait_ge(in_bin_ready, 1)
            rhs_slots(0, FIRST_SLOTS)
            pool.wait_ge(in_bin_ready, 2)
            rhs_slots(FIRST_SLOTS, NS)

            for pair in range(H // 2):
                pool.wait_ge(head_sums, 4 * (pair + 1))
                pool.tensor_scalar(inv_sum, inv_sum, TINY, None, ALU.max).then_inc(sums_kept, 1)
                pool.wait_ge(inverted, pair + 1)
                pool.tensor_tensor(heads_t[:, pair, :], heads_t[:, pair, :], inv_sum, ALU.mult).then_inc(head_done, 1)

        @block.scalar
        def _(act):
            act.dma_start(att_sb[:, :, :], att).then_inc(small_in, 16)
            act.dma_start(colv[:, :], cols).then_inc(small_in, 16)
            act.dma_start(x0[:, :, :], x.rearrange("(c p) n -> p c n", p=P)).then_inc(x_in, 16)
            act.dma_start(bv_row, rows[0:1, :].to_broadcast([P, C])).then_inc(small_in, 16)
            for i, w in enumerate((wq, wk, wv)):
                act.dma_start(wqkv[:, i], w.rearrange("(c p) n -> p c n", p=P)).then_inc(wqkv_in, 16)
            act.sem_inc(basis_ev, EV0)
            act.wait_ge(small_in, 48)
            act.activation(gate[:, 0, 0:1], colv[:, 0:1], ACT.Exp, scale=0.0).then_inc(table_in, 1)

            def root_of_variance(n, c):
                act.wait_ge(var_ready, NC * n + c + 1)
                act.activation(rstd[:, c:c + 1], rstd[:, c:c + 1], ACT.Sqrt).then_inc(std_ready, 1)

            def transposed_rows(to, bank, r, done, ev):
                act.wait_ge(done, r + 1)
                act.activation(to[:, :, r * P:(r + 1) * P], ps[:, bank + r, :].rearrange("p (c n) -> p c n", c=NC),
                               ACT.Copy).then_inc(ev, 1)

            def transposed_gained(to, r, gain, bias, done, ev):
                act.wait_ge(done, r + 1)
                for c in range(NC):
                    act.activation(to[:, c, r * P:(r + 1) * P], ps[:, r, c * P:(c + 1) * P], ACT.Identity,
                                   scale=colv[:, gain + c:gain + c + 1], bias=colv[:, bias + c:bias + c + 1]).then_inc(ev, 1)

            def basis_rows(half, n, turn):
                if turn is not None:
                    act.wait_ge(w_out[half], turn)
                for k in range(2):
                    act.wait_ge(basis_mm, n + (k + 1 + TILE0))
                    act.activation(wrows[:, half, k, :], ps[:, 4 + k, :], ACT.Copy).then_inc(basis_ev, 1)

            act.wait_ge(attr_in, 16)
            act.wait_ge(top_ready, 1)
            for part, e in enumerate((slice(0, FIRST), slice(FIRST, EC))):
                for h in range(H):
                    act.activation(weight_f[:, e, h:h + 1], attr_sb[:, e, h:h + 1], ACT.Exp,
                                   bias=bias_top[:, h:h + 1]).then_inc(weight_ready, 1)
                act.wait_ge(weight_ready, (H + 1) * part + H)
                act.activation(fields_b[:, e, 4:4 + H], weight_f[:, e], ACT.Copy).then_inc(weight_ready, 1)
            for half in range(2):
                basis_rows(half, 2 * half, None)
            for c in range(NC):
                root_of_variance(0, c)
            act.wait_ge(small_in, 48)
            for r in range(NC):
                transposed_gained(z_t, r, 0, 4, z_mm, z_ev)
            act.wait_ge(bq_ready, 1)
            act.wait_ge(consts, n_consts)
            for g in range(3 * NC):
                kind, m = divmod(g, NC)
                bank = QKV_BANKS[g % len(QKV_BANKS)]
                if kind < 2:
                    act.wait_ge(qk_mm, g + 1)
                if kind == 0:
                    for e in range(2):
                        own = slice(D * e, D * e + D)
                        act.activation(q_t[own, 2 * m + e, :], ps[own, bank, :], ACT.Identity, scale=-SCALE,
                                       bias=bq_scaled[own, m:m + 1]).then_inc(qk_ev, 1)
                elif kind == 1:
                    act.activation(k_t[:, m, :], ps[:, bank, :], ACT.Identity, bias=colv[:, 12 + m:13 + m]).then_inc(qk_ev, 1)
                n = RING + 2 * g
                basis_rows(g % 2, n, 64 * (n // RING))
            with act.Fori(*span(TILES - RING, 2 * TILES, 4)) as m:
                for half in range(2):
                    basis_rows(half, m + 2 * half, m * 16)

            for r in range(NC):
                transposed_rows(none, 0, r, none_mm, none_ev)
            def head_copy(h):
                e = h % 2
                mine, others = slice(D * e, D * e + D), slice(D * (1 - e), D * (1 - e) + D)
                act.wait_ge(value_mm, NC * (h + 1))
                act.activation(heads_t[mine, h // 2, :], ps[mine, 6 + e, :], ACT.Copy).then_inc(head_sums, 1)
                if h >= 2:
                    act.wait_ge(head_done, h // 2)
                act.activation(inv_sum[mine], ps[others, 6 + e, :], ACT.Copy).then_inc(head_sums, 1)

            for k in range(STEPS):
                h, r = divmod(k, NC)
                act.wait_ge(max_ready, k + 1)
                if h >= 2:
                    act.wait_ge(exp_mm, NC * (h - 1))
                act.activation(exps[:, h % 2, r, :], ps[:, r, :], ACT.Exp, scale=-1.0,
                               bias=neg_max[:, h, r:r + 1]).then_inc(exp_done, 1)
                if k > VALUE_LAG and (k - VALUE_LAG) % NC == 0:
                    head_copy((k - VALUE_LAG) // NC - 1)
            for h in range((STEPS - 1 - VALUE_LAG) // NC, H):
                head_copy(h)
            for c in range(NC + 2):
                if c < NC:
                    root_of_variance(1, c)
                if c >= 2:
                    transposed_gained(z2_t, c - 2, 16, 20, z2_mm, z2_ev)
            for g in range(2 * NH):
                half, m = divmod(g, NH)
                act.wait_ge(h1_mm, g + 1)
                act.activation(h1_t[:, m, half * HALF:(half + 1) * HALF], ps[:, 4 + m % 4, half * HALF:(half + 1) * HALF],
                               ACT.Silu, bias=colv[:, 24 + m:25 + m]).then_inc(h1_ev, 1)
            for c in range(NC + 1):
                if c < NC:
                    root_of_variance(2, c)
                if c >= 1:
                    transposed_rows(y_t, 4, c - 1, y_mm, y_ev)
            for layer in range(2):
                if layer == 1:
                    for r in range(NC):
                        transposed_rows(g1_t, 4, r, g1_mm, g1_ev)
                act.wait_ge(table_in, 1)
                act.wait_ge(gate_ready, layer + 1)
                act.activation(gate[:, :, :], gate_dot[:, :, :], ACT.Sigmoid).then_inc(gate_ev, 1)
                act.wait_ge(gate_ev, layer + 1)
                for g in range(TYPES * NC):
                    t, c = divmod(g, NC)
                    act.wait_ge(msg_mm, TYPES * NC * layer + g + 1)
                    act.activation(msgs[:, t, c, :], ps[:, 4 + c, :], ACT.Copy,
                                   scale=gate[:, c, t:t + 1]).then_inc(msg_ev, 1)
            for c in range(NC):
                root_of_variance(3, c)

        @block.vector
        def _(dve):
            count = [0]

            def step(ins):
                count[0] += 1
                ins.then_inc(dve_done, 1)
                dve.wait_ge(dve_done, count[0])

            dve.wait_ge(src_in, 16)
            dve.wait_ge(bin_const, 1)
            step(dve.tensor_scalar(src_hi, src_i, 4, None, ALU.logical_shift_right))
            step(dve.tensor_copy(bin_f, src_hi))
            step(dve.tensor_tensor(onehot_bin, bin_f.unsqueeze(1).to_broadcast([P, NBIN, EC]),
                                   iota_bin[:, :].unsqueeze(2).to_broadcast([P, NBIN, EC]), ALU.is_equal))
            flat_oh = onehot_bin.rearrange("p b e -> p (b e)")
            flat_run = running.rearrange("p b e -> p (b e)")
            step(dve.tensor_tensor_scan(flat_run, flat_oh, flat_oh, 0.0, ALU.add, ALU.max))
            step(dve.memset(bin_cum[:, 0:1], 0.0))
            step(dve.memset(bin_base[:, 0:1], 0.0))
            step(dve.tensor_copy(bin_cum[:, 1:NBIN + 1], running[:, :, EC - 1:EC].rearrange("p b e -> p (b e)")))
            dve.tensor_tensor(bin_cnt[:, :], bin_cum[:, 1:NBIN + 1], bin_cum[:, 0:NBIN], ALU.subtract).then_inc(cnt_ready, 1)
            dve.wait_ge(attr_in, 16)
            dve.tensor_reduce(bias_max[:, :], attr_sb.rearrange("p e h -> p h e"), AX, ALU.max).then_inc(pmax_ready, 1)

            dve.wait_ge(cnt_mm, 1)
            step(dve.tensor_scalar(bin_pairs_i[:, :], ps[:, 7, NBIN:2 * NBIN], float(GROUP - 1), None, ALU.add))
            step(dve.tensor_scalar(bin_pairs_s[:, :], bin_pairs_i[:, :], 8, None, ALU.logical_shift_right))
            step(dve.tensor_copy(bin_pairs[:, :], bin_pairs_s[:, :]))
            step(dve.tensor_tensor_scan(bin_base[:, 1:NBIN + 1], bin_pairs[:, :], bin_pairs[:, :], 0.0, ALU.add, ALU.max))
            step(dve.scalar_tensor_tensor(bin_off[:, :], bin_base[:, 0:NBIN], float(GROUP), ps[:, 7, 0:NBIN], ALU.mult, ALU.add))
            dve.sem_inc(bins_read, 1)
            step(dve.scalar_tensor_tensor(bin_off[:, :], bin_off[:, :], -1.0, bin_cum[:, 0:NBIN], ALU.add, ALU.subtract))

            def edge_places(e, n):
                here = places[:, :, 0:n]
                step(dve.tensor_tensor(here, running[:, :, e], bin_off.unsqueeze(2).to_broadcast([P, NBIN, n]), ALU.add))
                step(dve.tensor_tensor(here, here, onehot_bin[:, :, e], ALU.mult))
                step(dve.tensor_reduce(pos[:, e], here.rearrange("p b e -> p e b"), AX, ALU.add))
                step(dve.tensor_copy(pos_i[:, e], pos[:, e]))
                step(dve.tensor_scalar(pos_lo[:, e], pos_i[:, e], P - 1, None, ALU.bitwise_and))
                step(dve.tensor_scalar(pos_hi[:, e], pos_i[:, e], 7, None, ALU.logical_shift_right))
                dve.scalar_tensor_tensor(edge_idx[:, e], pos_lo[:, e], float(NS), pos_hi[:, e],
                                         ALU.mult, ALU.add).then_inc(idx_ready, 1)

            dve.tensor_scalar(src_lo, src_i, BIN - 1, None, ALU.bitwise_and).then_inc(src_lo_ready, 1)
            edge_places(slice(0, FIRST), FIRST)

            def norm(n, v, to, ready, arrive, lag):
                for c in range(NC + lag):
                    if c < NC:
                        arrive(c)
                        step(dve.bn_stats(stats[:, c, :], v[:, c, :]))
                        step(dve.bn_aggr(mv[:, c, :], stats[:, c, :]))
                        dve.tensor_scalar(rstd[:, c:c + 1], mv[:, c, 1:2], EPS, None, ALU.add).then_inc(var_ready, 1)
                    d = c - lag
                    if d >= 0:
                        dve.wait_ge(std_ready, NC * n + d + 1)
                        step(dve.reciprocal(rstd[:, d:d + 1], rstd[:, d:d + 1]))
                        dve.tensor_scalar(to[:, d, :], v[:, d, :], mv[:, d, 0:1], rstd[:, d:d + 1], ALU.subtract, ALU.mult)\
                           .then_inc(ready, 1)

            dve.wait_ge(consts, early_consts)
            step(dve.tensor_scalar(group_diff[:, :, :], group_diff[:, :, :], GROUPS - 1, None, ALU.bitwise_and))
            step(dve.tensor_scalar(group_mask[:, :, :], group_diff[:, :, :], 0.0, None, ALU.is_equal))
            dve.wait_ge(small_in, 48)
            for layer in range(2):
                dve.tensor_tensor(
                    att_blk[0:BP, layer, 0:TYPES * GROUPS].rearrange("p (t g) -> p t g", t=TYPES), group_mask[0:BP, :, :],
                    att_sb[:, layer, :].unsqueeze(2).to_broadcast([BP, TYPES, GROUPS]), ALU.mult).then_inc(att_ready, 1)
            dve.tensor_scalar(bq_scaled[:, :], colv[:, 8:12], -SCALE, None, ALU.mult).then_inc(bq_ready, 1)

            dve.wait_ge(x_in, 16)
            norm(0, x0, z, z_ready, lambda c: None, 1)

            edge_places(slice(FIRST, EC), EC - FIRST)
            dve.wait_ge(edges_in, 32)
            dve.wait_ge(src_lo_ready, 1)
            dve.wait_ge(weight_ready, 2 * (H + 1))
            edge_fields(dve, slice(FIRST, EC), dve_fields, 0, fields_ready)

            dve.wait_ge(consts, n_consts)

            cmp = dense[0:1, 0:PAIRS * NBIN].rearrange("p (s b) -> p s b", b=NBIN)
            dve.wait_ge(idx_ready, 2)
            step(dve.tensor_tensor(cmp, bin_base[0:1, 0:NBIN].unsqueeze(1).to_broadcast([1, PAIRS, NBIN]),
                                   iota_pair[:, :].unsqueeze(2).to_broadcast([1, PAIRS, NBIN]), ALU.is_le))
            pair_f = dense[0:1, PAIRS * NBIN:PAIRS * NBIN + PAIRS]
            step(dve.tensor_reduce(pair_f, cmp, AX, ALU.add))
            step(dve.tensor_scalar(pair_off[:, :], pair_f, -1.0, float(BIN), ALU.add, ALU.mult))

            for c in range(NC):
                dve.wait_ge(v_mm, c + 1)
                dve.tensor_tensor(v1[:, c, :, 0:3:2, :], ps[:, QKV_BANKS[(2 * NC + c) % len(QKV_BANKS)], :].rearrange("p (m e d) -> p m e d", e=2, d=D),
                                  bv_row.rearrange("p (m e d) -> p m e d", e=2, d=D), ALU.add).then_inc(v_ev, 1)

            dve.wait_ge(v_ev, NC)
            dve.wait_ge(pool_done, 1 + 7)
            step(dve.memset(dense[:, :], 0.0))

            def place_in_bin(start, end):
                n = end - start
                dve.tensor_tensor(in_bin[:, start:end, :], edges[:, start:end, 1:2].to_broadcast([P, n, BIN]),
                                  iota_src[:, :].unsqueeze(1).to_broadcast([P, n, BIN]), ALU.is_equal).then_inc(in_bin_ready, 1)

            def target(s, k):
                dve.tensor_scalar(targets[:, k, :], iota_node[:, :], edges[:, bass.ds(s, 1), 0:1].rearrange("p s f -> p (s f)"),
                                  None, ALU.is_equal).then_inc(target_ready, 1)

            dve.sem_inc(slot_added, ADDED0)
            dve.wait_ge(first_in, 16)
            place_in_bin(0, FIRST_SLOTS)
            for k in range(AHEAD):
                target(k, k)
            dve.wait_ge(sorted_in, 16)
            place_in_bin(FIRST_SLOTS, NS)
            step(dve.memset(edges[:, NS:NS + AHEAD, :], 0.0))
            dve.wait_ge(in_bin_ready, 2)
            with dve.Fori(*span(0, NS, DVE_SLOTS)) as s:
                for k in range(0, DVE_SLOTS, 2):
                    for j in range(k + AHEAD, k + AHEAD + 2):
                        target(s + j, j % SLOT_RING)
                    if k % 8 == DVE_TURN:
                        slot_rhs(dve, s, k - DVE_TURN + 7).then_inc(last_rhs_ready, 1)
                    offset = dve.value_load(pair_off[0:1, bass.ds(s // 2 + k // 2, 1)], min_val=0, max_val=N - BIN)
                    dve.wait_ge(slot_mm, s + (k + 2 + MM0))
                    dve.wait_ge(slot_added, s + (k + ADDED0))
                    to = mats.rearrange("p c a r -> p (c a) r")[:, :, bass.ds(offset, BIN)]\
                        .rearrange("p (b a) r -> p b a r", b=2)
                    bank = k % 4
                    got = ps[:, bank:bank + 2, 0:2 * HI_W].rearrange("p b (a r) -> p b a r", r=BIN)
                    dve.tensor_tensor(to, got, to, ALU.add).then_inc(slot_added, 2)
            dve.wait_ge(slot_added, NS + ADDED0)

            for c in range(NC):
                step(dve.tensor_tensor(none_t[:, c, :], mats[:, c, H, :], mats[:, c, H + 1, :], ALU.add))
                dve.tensor_scalar(none_t[:, c, :], none_t[:, c, :], 0.0, NO_EDGE, ALU.is_equal, ALU.mult).then_inc(none_ready, 1)

            def largest(k):
                h, r = divmod(k, NC)
                dve.wait_ge(score_mm, k + 1)
                dve.tensor_tensor_reduce(out=ps[:, r, :], in0=ps[:, r, :], in1=none[:, r, :], scale=1.0, scalar=NO_EDGE,
                                         op0=ALU.add, op1=ALU.min, accum_out=neg_max[:, h, r:r + 1]).then_inc(max_ready, 1)

            def prob(k):
                h, c = divmod(k, NC)
                dve.wait_ge(exp_mm, k + 1)
                if h >= 1:
                    dve.wait_ge(value_mm, k + 1 - NC)
                dve.tensor_tensor(probs[:, c, :], ps[:, 4 + k % 2, :], mats[:, c, h, :], ALU.mult).then_inc(prob_done, 1)

            def invert(pair, part):
                dve.wait_ge(sums_kept, pair + 1)
                own = inv_sum[:, part * P:(part + 1) * P]
                step(dve.reciprocal(own, own))
                if part == NC - 1:
                    dve.sem_inc(inverted, 1)

            dve.wait_ge(none_ev, NC)
            for k in range(STEPS + INVERT_LAG - NC):
                if k < STEPS:
                    largest(k)
                if 0 <= k - EXP_LAG < STEPS:
                    prob(k - EXP_LAG)
                pair, part = divmod(k - INVERT_LAG, 2 * NC)
                if pair >= 0 and part < NC:
                    invert(pair, part)
                if k == STEPS + EXP_LAG:
                    dve.wait_ge(late_in, 16)
                c = k - STEPS - EXP_LAG
                if 0 <= c < NC:
                    step(dve.tensor_tensor(x0[:, c, :], x0[:, c, :], row4[:, 0, :], ALU.add))

            def bring_x1(c):
                dve.wait_ge(x1_mm, c + 1)
                step(dve.tensor_tensor(x1[:, c, :], ps[:, 4 + c, :], x0[:, c, :], ALU.add))

            norm(1, x1, z2, z2_ready, bring_x1, 1)
            for c in range(NC):
                step(dve.tensor_tensor(x0[:, c, :], x0[:, c, :], row4[:, 0, :], ALU.subtract))
                step(dve.tensor_tensor(x0[:, c, :], x0[:, c, :], x1[:, c, :], ALU.add))
                step(dve.tensor_tensor(x0[:, c, :], x0[:, c, :], row4[:, 1, :], ALU.add))

            def bring_x2(c):
                dve.wait_ge(x2_mm, c + 1)
                step(dve.tensor_tensor(x0[:, c, :], ps[:, c, :], x0[:, c, :], ALU.add))

            norm(2, x0, y, y_ready, bring_x2, 0)

            def gate_dots(layer, v, c):
                for t in range(TYPES):
                    ins = dve.tensor_tensor_reduce(out=junk[:, t, :], in0=v[:, c, :], in1=gate_rows[:, TYPES * layer + t, :],
                                                   scale=1.0, scalar=0.0, op0=ALU.mult, op1=ALU.add,
                                                   accum_out=gate_dot[:, c, t:t + 1])
                    if (c, t) == (NC - 1, TYPES - 1):
                        ins.then_inc(gate_ready, 1)
                    else:
                        step(ins)

            dve.wait_ge(gates_in, 16)
            dve.wait_ge(y_ready, NC)
            for c in range(NC):
                gate_dots(0, y, c)
            for c in range(NC):
                dve.wait_ge(agg_mm, c + 1)
                step(dve.tensor_tensor(g1_out[:, c, :], ps[:, c, :], row4[:, 2, :], ALU.add))
                dve.tensor_scalar(g1_out[:, c, :], g1_out[:, c, :], 0.0, None, ALU.max).then_inc(g1_ready, 1)
                dve.wait_ge(g1_ready, c + 1)
                if c == 0:
                    dve.wait_ge(gate_ev, 1)
                gate_dots(1, g1_out, c)
            for c in range(NC):
                step(dve.tensor_tensor(y[:, c, :], y[:, c, :], row4[:, 3, :], ALU.add))

            def bring_out(c):
                dve.wait_ge(agg_mm, NC + c + 1)
                step(dve.tensor_tensor(x0[:, c, :], ps[:, c, :], y[:, c, :], ALU.add))

            norm(3, x0, g1_out, out_ready, bring_out, 0)

        @block.tensor
        def _(pe):
            mm = nc.tensor.matmul

            def transpose_rows(v, r, bank, ready, done):
                pe.wait_ge(ready, r + 1)
                for c in range(NC):
                    last = nc.tensor.transpose(ps[:, bank + r, c * P:(c + 1) * P], v[:, r, c * P:(c + 1) * P], ident[:, :])
                last.then_inc(done, 1)

            def product(bank, pairs, done=None, start=True, stop=True):
                for i, (l, r) in enumerate(pairs):
                    last = mm(ps[:, bank, :], l, r, start=start and i == 0, stop=stop and i == len(pairs) - 1)
                if done is not None:
                    last.then_inc(done, 1)

            def then_transposes(make, follow, v, bank, ready, done):
                for n in range(NC):
                    make(n)
                    if n >= 1:
                        transpose_rows(v, n - 1, bank, ready, done)
                for n in range(NC):
                    follow(n)
                    if n == 0:
                        transpose_rows(v, NC - 1, bank, ready, done)

            def basis_tile(layer, k, n, turn):
                pe.wait_ge(basis_in[k], turn)
                pe.wait_ge(basis_ev, n + 1)
                for j in range(TILE_ROWS):
                    last = mm(ps[32 * j:32 * j + 32, 4 + k % 2, :], att_blk[0:BP, layer, :],
                              ring[0:BP, k, j * C:(j + 1) * C], start=True, stop=True)
                last.then_inc(basis_mm, 1)

            pe.sem_inc(basis_mm, TILE0)
            pe.sem_inc(slot_mm, MM0)
            pe.wait_ge(consts, early_consts)
            pe.wait_ge(cnt_ready, 1)
            mm(ps[:, 7, 0:NBIN], tri[:, :], bin_cnt[:, :], start=True, stop=True)
            mm(ps[:, 7, NBIN:2 * NBIN], ones[:, :], bin_cnt[:, :], start=True, stop=True).then_inc(cnt_mm, 1)
            pe.wait_ge(att_ready, 2)
            for n in range(RING):
                basis_tile(0, n, n, 16)
            for r in range(NC):
                transpose_rows(z, r, 0, z_ready, z_mm)
            pe.wait_ge(wqkv_in, 48)
            pe.wait_ge(z_ev, NC * NC)
            pe.wait_ge(bins_read, 1)
            for g in range(3 * NC):
                kind, m = divmod(g, NC)
                bank = QKV_BANKS[g % len(QKV_BANKS)]
                if g >= len(QKV_BANKS):
                    f = g - len(QKV_BANKS)
                    pe.wait_ge(qk_ev, 2 * (f + 1) if f < NC else NC + f + 1)
                own = slice(m * P, (m + 1) * P)
                if kind < 2:
                    product(bank, [(wqkv[:, kind, c, own], z_t[:, c, :]) for c in range(NC)], qk_mm)
                else:
                    product(bank, [(z_t[:, c, own], wqkv[:, 2, c, :]) for c in range(NC)], v_mm)
                for n in range(RING + 2 * g, RING + 2 * g + 2):
                    basis_tile(0, n % RING, n, 16 * (n // RING + 1))
            for n in range(TILES - RING, TILES):
                basis_tile(0, n % RING, n, 16 * (n // RING + 1))
            with pe.Fori(*span(TILES, 2 * TILES - TILED // RING, RING)) as m:
                for k in range(RING):
                    basis_tile(1, k, m + k, m * (16 // RING) + 16)
            pe.wait_ge(qk_ev, 3 * NC)
            pe.wait_ge(v_ev, NC)

            def slot(s, k):
                pe.wait_ge(target_ready, s + (k + 1))
                if k % 8 == 7:
                    pe.wait_ge(last_rhs_ready, s // 8 + (k // 8 + 1))
                else:
                    pe.wait_ge(rhs_ready, s + (k + 1))
                if k % 2 == 0:
                    pe.wait_ge(slot_added, s + (k + 2))
                for c in range(NC):
                    bank = k // 2 % 2 * 2 + c // 2
                    o = ps[:, bank, HI_W * (c % 2):HI_W * (c % 2) + HI_W]
                    t = targets[:, k % SLOT_RING, c * P:(c + 1) * P]
                    mm(o, t, rhs[:, k % SLOT_RING, 0:HI_W], start=k % 2 == 0 and c % 2 == 0, stop=False)
                    mm(o[:, 0:LO_W], t, rhs[:, k % SLOT_RING, HI_W:HI_W + LO_W], start=False, stop=False)
                    last = mm(o[:, 0:LO_W], t, rhs[:, k % SLOT_RING, HI_W + LO_W:RHS_W], start=False,
                              stop=k % 2 == 1 and c % 2 == 1)
                last.then_inc(slot_mm, 1)

            with pe.Fori(*span(0, TILED, SLOT_TURN)) as s:
                for k in range(SLOT_TURN):
                    slot(s, k)
                    if k % 4 == 3:
                        t = k // 4
                        first = 2 * TILES - TILED // RING
                        basis_tile(1, t, s // (SLOT_TURN // RING) + (first + t), s + (first * 16 // RING + 16))
            with pe.Fori(*span(TILED, NS, 8)) as s:
                for k in range(8):
                    slot(s, k)

            pe.wait_ge(slot_added, NS + ADDED0)
            for r in range(NC):
                transpose_rows(none_t, r, 0, none_ready, none_mm)
            pe.wait_ge(basis_ev, 2 * TILES + EV0)

            def scores(k):
                h, r = divmod(k, NC)
                if h == 0:
                    pe.wait_ge(none_ev, r + 1)
                else:
                    pe.wait_ge(exp_done, k + 1 - NC)
                mm(ps[:, r, :], q_t[:, h, r * P:(r + 1) * P], k_t[:, h // 2, :], start=True, stop=True).then_inc(score_mm, 1)

            def transpose_exps(k):
                h, c = divmod(k, NC)
                pe.wait_ge(exp_done, NC * (h + 1))
                if k >= 2:
                    pe.wait_ge(prob_done, k - 1)
                for r in range(NC):
                    last = nc.tensor.transpose(ps[:, 4 + k % 2, r * P:(r + 1) * P], exps[:, h % 2, r, c * P:(c + 1) * P],
                                               ident[:, :])
                last.then_inc(exp_mm, 1)

            def values(k):
                h, c = divmod(k, NC)
                pe.wait_ge(prob_done, k + 1)
                if h >= 2 and c == 0:
                    pe.wait_ge(head_sums, 2 * (h - 1))
                mm(ps[:, 6 + h % 2, :], v1[:, c, h // 2, h % 2:h % 2 + 2, :].rearrange("p a d -> p (a d)"), probs[:, c, :],
                   start=c == 0, stop=c == NC - 1).then_inc(value_mm, 1)

            for k in range(STEPS + VALUE_LAG):
                if k < STEPS:
                    scores(k)
                if 0 <= k - EXP_LAG < STEPS:
                    transpose_exps(k - EXP_LAG)
                if k >= VALUE_LAG:
                    values(k - VALUE_LAG)

            pe.wait_ge(wo_in, 16)
            pe.wait_ge(head_done, H // 2 - 1)
            pe.wait_ge(head_sums, 2 * H)
            for n in range(NC):
                product(4 + n, [(heads_t[:, c, n * P:(n + 1) * P], wo_sb[:, c, :]) for c in range(NC - 1)], stop=False)
            pe.wait_ge(head_done, H // 2)
            for n in range(NC):
                product(4 + n, [(heads_t[:, NC - 1, n * P:(n + 1) * P], wo_sb[:, NC - 1, :])], x1_mm, start=False)
            for r in range(NC):
                transpose_rows(z2, r, 0, z2_ready, z2_mm)
            pe.wait_ge(w1_in, 16)
            for half in range(2):
                own = slice(half * HALF, (half + 1) * HALF)
                pe.wait_ge(z2_ev, NC * NC * (half + 1) // 2)
                for m in range(NH):
                    g = NH * half + m
                    if g >= 4:
                        pe.wait_ge(h1_ev, g - 3)
                    for c in range(NC):
                        last = mm(ps[:, 4 + m % 4, own], w1_sb[:, c, m * P:(m + 1) * P], z2_t[:, c, own],
                                  start=c == 0, stop=c == NC - 1)
                    last.then_inc(h1_mm, 1)
            pe.wait_ge(w2_in, 16 * NC)

            def feed_forward(n):
                pe.wait_ge(h1_ev, NH * (n // 2 + 1))
                product(n, [(h1_t[:, m, n * P:(n + 1) * P], w2_sb[:, m // 2, m % 2, :]) for m in range(NH)], x2_mm)

            def root_product(layer):
                in_t, ev = ((y_t, y_ev), (g1_t, g1_ev))[layer]
                root, loaded = ((root_a, wa_in), (root_b, wb_in))[layer]

                def make(n):
                    if n == 0:
                        pe.wait_ge(loaded, 16 * (NC + 1))
                    pe.wait_ge(ev, n + 1)
                    product(n, [(in_t[:, c, n * P:(n + 1) * P], root[:, c, :]) for c in range(NC)], stop=False)
                return make

            def messages_and_sums(layer):
                in_t, w = ((y_t, w_a), (g1_t, w_b))[layer]
                for g in range(TYPES * NC):
                    t, n = divmod(g, NC)
                    if g >= 4:
                        pe.wait_ge(msg_ev, TYPES * NC * layer + g - 3)
                    product(4 + n, [(in_t[:, c, n * P:(n + 1) * P], w[:, c, t, :]) for c in range(NC)], msg_mm)
                pe.wait_ge(msg_ev, TYPES * NC * (layer + 1))
                return lambda n: product(n, [(mats[:, c, H + t, n * P:(n + 1) * P], msgs[:, t, c, :]) for t in range(TYPES)
                                             for c in range(NC)], agg_mm, start=False)

            then_transposes(feed_forward, root_product(0), y, 4, y_ready, y_mm)
            aggregate = messages_and_sums(0)
            then_transposes(aggregate, root_product(1), g1_out, 4, g1_ready, g1_mm)
            aggregate = messages_and_sums(1)
            for n in range(NC):
                aggregate(n)


def kernel(**inputs):
    import numpy as np
    import concourse.bacc as bacc
    from concourse.bass_utils import run_bass_kernel_spmd

    def a(name):
        return np.ascontiguousarray(np.asarray(inputs[name]))

    def column(v):
        return v.reshape(-1, P).T

    gates = np.concatenate([a(f"L1_gnn_gate_w{i}").reshape(TYPES, C) for i in (1, 2)])
    att = np.stack([np.repeat(a(f"L1_gnn_att{i}").T, GROUPS, axis=0) for i in (1, 2)], axis=1)
    arrays = {
        "x": a("x"), "src": a("src").reshape(P, EC), "dst": a("dst").reshape(P, EC),
        "etype": a("edge_type_2").reshape(P, EC), "attr": a("edge_attr_8").reshape(P, EC, H),
        "cols": np.concatenate([column(a(n)) for n in COLS], axis=1),
        "rows": np.stack([a(n) for n in ROWS]),
        "wq": a("L0_gnn_Wq"), "wk": a("L0_gnn_Wk"), "wv": a("L0_gnn_Wv"), "wo": a("L0_gnn_Wo"),
        "w1": a("L0_gnn_W1"), "w2": a("L0_gnn_W2"),
        "basis1": a("L1_gnn_basis1"), "basis2": a("L1_gnn_basis2"), "att": att,
        "gates": gates, "root1": a("L1_gnn_root1"), "root2": a("L1_gnn_root2"),
    }
    arrays = {k: np.ascontiguousarray(v) for k, v in arrays.items()}
    nc = bacc.Bacc("TRN2", target_bir_lowering=False, num_devices=1)
    t = {k: nc.dram_tensor(k, v.shape, mybir.dt.from_np(v.dtype), kind="ExternalInput").ap() for k, v in arrays.items()}
    out = nc.dram_tensor("out", (N, C), F32, kind="ExternalOutput").ap()
    build(nc, t["x"], t["src"], t["dst"], t["etype"], t["attr"], t["cols"], t["rows"], t["wq"], t["wk"], t["wv"],
          t["wo"], t["w1"], t["w2"], [t["basis1"], t["basis2"]], t["att"], t["gates"], [t["root1"], t["root2"]], out)
    r = run_bass_kernel_spmd(nc, [arrays], core_ids=[0])
    return r.results[0]["out"]
```
